# Optimizing a Trainium2 kernel written in Bass

```python
import numpy as np
import jax
import jax.numpy as jnp

def _softmax(x, axis=-1):
    return jax.nn.softmax(x, axis=axis)

def _gelu(x):
    return jax.nn.gelu(x, approximate=True)

def _silu(x):
    return jax.nn.silu(x)

def _sigmoid(x):
    return jax.nn.sigmoid(x)

def _layernorm(x, axis=-1, eps=1e-05):
    m = jnp.mean(x, axis=axis, keepdims=True)
    v = jnp.var(x, axis=axis, keepdims=True)
    return (x - m) / jnp.sqrt(v + eps)

def _scatter_add(tgt, idx, src, axis=0):
    return tgt.at[idx].add(src)

def _segment_sum(src, seg, n):
    return jax.ops.segment_sum(src, seg, n)
kernel_name = 'mk_gnn_resnorm_d1_gnn_r8_5acdc9'

def setup_inputs(seed: int=0):
    np.random.seed(seed)
    _w = jnp.asarray

    def _rec_inputs():
        import jax
        import jax.numpy as jnp
        _gk = jax.random.key(seed)
        x = -8.776e-05 + 1 * jax.random.normal(jax.random.fold_in(_gk, 1), (12500, 256), jnp.float32)
        src = jax.random.randint(jax.random.fold_in(_gk, 2), (200000,), 0, 12500, jnp.int32)
        dst = jax.random.randint(jax.random.fold_in(_gk, 3), (200000,), 0, 12500, jnp.int32)
        _o = jnp.argsort(dst, stable=True)
        src = src[_o]
        dst = dst[_o]
        return (x, src, dst)
    x, src, dst = _rec_inputs()

    def _L0_gnn_setup():
        import math
        import jax, jax.numpy as jnp
        import numpy as np
        N = 2500
        E = 40000
        D_IN = 256
        D_OUT = 256
        H = 8
        DK = D_OUT // H
        key = jax.random.key(seed)
        ks = jax.random.split(key, 16)
        h = jax.random.normal(ks[0], (N, D_IN), dtype=jnp.float32)
        src = jax.random.randint(ks[1], (E,), 0, N, dtype=jnp.int32)
        dst = jax.random.randint(ks[2], (E,), 0, N, dtype=jnp.int32)
        s = 1.0 / math.sqrt(D_IN)
        Wk = jax.random.uniform(ks[3], (D_OUT, D_IN), jnp.float32, -s, s)
        bk = jnp.zeros((D_OUT,), jnp.float32)
        Wq = jax.random.uniform(ks[4], (D_OUT, D_IN), jnp.float32, -s, s)
        bq = jnp.zeros((D_OUT,), jnp.float32)
        Wv = jax.random.uniform(ks[5], (D_OUT, D_IN), jnp.float32, -s, s)
        bv = jnp.zeros((D_OUT,), jnp.float32)
        so = 1.0 / math.sqrt(D_OUT)
        Wa = jax.random.uniform(ks[6], (D_OUT, D_OUT), jnp.float32, -so, so)
        ba = jnp.zeros((D_OUT,), jnp.float32)
        bound = math.sqrt(6.0 / (DK + DK))
        rel_att = jax.random.uniform(ks[7], (H, DK, DK), jnp.float32, -bound, bound)
        rel_msg = jax.random.uniform(ks[8], (H, DK, DK), jnp.float32, -bound, bound)
        rel_pri = jnp.ones((H,), jnp.float32)
        skip = jnp.ones((), jnp.float32)
        return {'h': h, 'src': src, 'dst': dst, 'Wk': Wk, 'bk': bk, 'Wq': Wq, 'bq': bq, 'Wv': Wv, 'bv': bv, 'Wa': Wa, 'ba': ba, 'rel_att': rel_att, 'rel_msg': rel_msg, 'rel_pri': rel_pri, 'skip': skip}
    _L0_gnn_all = _L0_gnn_setup()
    _L0_gnn_in = {k: v for k, v in _L0_gnn_all.items() if k in ('Wk', 'bk', 'Wq', 'bq', 'Wv', 'bv', 'Wa', 'ba', 'rel_att', 'rel_msg', 'rel_pri', 'skip')}
    del _L0_gnn_all
    return {'x': x, 'src': src, 'dst': dst, 'L0_gnn_Wk': _L0_gnn_in['Wk'], 'L0_gnn_bk': _L0_gnn_in['bk'], 'L0_gnn_Wq': _L0_gnn_in['Wq'], 'L0_gnn_bq': _L0_gnn_in['bq'], 'L0_gnn_Wv': _L0_gnn_in['Wv'], 'L0_gnn_bv': _L0_gnn_in['bv'], 'L0_gnn_Wa': _L0_gnn_in['Wa'], 'L0_gnn_ba': _L0_gnn_in['ba'], 'L0_gnn_rel_att': _L0_gnn_in['rel_att'], 'L0_gnn_rel_msg': _L0_gnn_in['rel_msg'], 'L0_gnn_rel_pri': _L0_gnn_in['rel_pri'], 'L0_gnn_skip': _L0_gnn_in['skip']}

def reference(x, src, dst, L0_gnn_Wk, L0_gnn_bk, L0_gnn_Wq, L0_gnn_bq, L0_gnn_Wv, L0_gnn_bv, L0_gnn_Wa, L0_gnn_ba, L0_gnn_rel_att, L0_gnn_rel_msg, L0_gnn_rel_pri, L0_gnn_skip):
    import jax
    import jax.numpy as jnp

    def _L0_gnn_ref(h, src, dst, Wk, bk, Wq, bq, Wv, bv, Wa, ba, rel_att, rel_msg, rel_pri, skip):
        import math
        import jax, jax.numpy as jnp
        import numpy as np
        N = 2500
        E = 40000
        D_IN = 256
        D_OUT = 256
        H = 8
        DK = D_OUT // H
        n = h.shape[0]
        sqrt_dk = math.sqrt(DK)
        k = (h @ Wk.T + bk).reshape(n, H, DK)
        q = (h @ Wq.T + bq).reshape(n, H, DK)
        v = (h @ Wv.T + bv).reshape(n, H, DK)
        k = jnp.einsum('nhd,hde->nhe', k, rel_att)
        v = jnp.einsum('nhd,hde->nhe', v, rel_msg)
        score = jnp.einsum('ehd,ehd->eh', q[dst], k[src]) * rel_pri / sqrt_dk
        m = jax.ops.segment_max(score, dst, num_segments=n)
        ex = jnp.exp(score - m[dst])
        z = jax.ops.segment_sum(ex, dst, num_segments=n)
        attn = ex / z[dst]
        agg = jax.ops.segment_sum(v[src] * attn[:, :, None], dst, num_segments=n)
        t = agg.reshape(n, D_OUT)
        trans = t @ Wa.T + ba
        alpha = jax.nn.sigmoid(skip)
        return trans * alpha + h * (1.0 - alpha)
    x = _layernorm(x + _L0_gnn_ref(x, src, dst, L0_gnn_Wk, L0_gnn_bk, L0_gnn_Wq, L0_gnn_bq, L0_gnn_Wv, L0_gnn_bv, L0_gnn_Wa, L0_gnn_ba, L0_gnn_rel_att, L0_gnn_rel_msg, L0_gnn_rel_pri, L0_gnn_skip), axis=-1)
    return x

_drawn_inputs = setup_inputs


def setup_inputs(seed=0):
    import zlib

    import numpy as np

    out = dict(_drawn_inputs(seed))
    spreads = {'L0_gnn_bk': (0.0, 0.8),
     'L0_gnn_bq': (0.0, 0.8),
     'L0_gnn_bv': (0.0, 0.1),
     'L0_gnn_ba': (0.0, 0.1),
     'L0_gnn_rel_pri': (1.0, 0.6)}
    factors = {'L0_gnn_Wk': 2.964, 'L0_gnn_Wq': 2.983, 'L0_gnn_rel_att': 3.001}
    for name, (base, spread) in spreads.items():
        noise = np.random.default_rng([zlib.crc32(name.encode()), seed]).standard_normal(out[name].shape)
        drawn = base * np.exp(spread * noise) if base else spread * noise
        out[name] = jnp.asarray(drawn.astype(out[name].dtype))
    for name, factor in factors.items():
        out[name] = (out[name] * factor).astype(out[name].dtype)
    return out
```

```python
from contextlib import ExitStack
import math

import concourse.bass as bass
from concourse import mybir

ALU = mybir.AluOpType
ACT = mybir.ActivationFunctionType
AX = mybir.AxisListType
F32 = mybir.dt.float32
I32 = mybir.dt.int32

P = 128
G = 17
C = P * G
BIG = 1e30
FAR = float(1 << 22)
EPS = 1e-5
PAIRS = [(g, min(2, G - g)) for g in range(0, G, 2)]
NQ = len(PAIRS)
WGROUPS = [(0, 4), (4, 4), (8, 4), (12, 5)]
TGROUPS = [(g, min(4, G - g)) for g in range(0, G, 4)]
NT = len(TGROUPS)


class Chunk:

    def __init__(self, turn, off):
        self.turn, self.off, self.par = turn, off, off % 2

    def done(self, per=1, credit=0, back=0):
        return self.turn * (2 * per) + ((self.off + 1) * per + credit - back)

    def landed(self, per=16):
        return self.turn * per + (self.off // 2 + 1) * per

    def number(self):
        return self.turn * 2 + self.off

    def next(self):
        return Chunk(self.turn, self.off + 1)

    def prev(self):
        return Chunk(self.turn, self.off - 1)


def gnn_program(nc, x, src, dst, Wk, bk, Wq, bq, Wv, bv, Wa, ba, rel_att, rel_msg, rel_pri, skip, out):
    N, D = x.shape
    E = src.shape[0]
    H, DK, _ = rel_att.shape
    HPB = P // DK
    assert D == 2 * P and H * DK == D and H == 8
    NW = len(WGROUPS)
    W = -(-N // P)
    ROWS = 125
    RC = E // ROWS
    assert ROWS * RC == E and W + 1 <= P
    J = E // C + 1
    SM = 2 * ((W + J + 6) // 2)
    assert SM <= 512
    TAIL = 16 * (-(-(4 * C + 16) // 16))
    EP = 1 + E + TAIL
    NPAIR = -(-N // (2 * P))
    PL = NPAIR // 2
    assert NPAIR == 2 * PL + 1

    with ExitStack() as ctx:
        def sb(name, shape, dt=F32):
            return ctx.enter_context(nc.sbuf_tensor(name, shape, dt))

        def sem(name):
            return ctx.enter_context(nc.semaphore(name))

        kv_dram = nc.dram_tensor("kv_rows", (N, 2 * D), F32, kind="Internal").ap()
        src_pad = nc.dram_tensor("src_pad", (EP,), I32, kind="Internal").ap()
        dst_pad = nc.dram_tensor("dst_pad", (EP,), I32, kind="Internal").ap()

        bank = [ctx.enter_context(nc.psum_tensor(f"bank{i}", [P, 512], F32)) for i in range(8)]
        ps_t = bank[0:2]
        ps_q = bank[2:4]
        ps_agg = bank[4]
        ps_small = bank[5]
        ps_fin = bank[6]
        ps_win = bank[7]
        MAXE = ps_small[:, 0:G * H]
        TAILT = ps_small[0:H, 136:264]
        CARRYT = ps_small[:, 264:392]
        CARRY = CARRYT[:, 0:H]
        NMAX = ps_small[:, 400:409]

        ident = sb("ident", [P, P])
        wv = sb("wv", [P, G, H, DK + 1])
        wl = bass.AP(wv, 0, [[G * H * (DK + 1), P], [2 * D, 4], [D, 2], [1, D]])
        rfold = sb("rfold", [P, 3, 2, P])
        bcol = sb("bcol", [P, 4, 2])
        bwide = sb("bwide", [P, 4, 2, P])
        pcol = sb("pcol", [P, 2])
        wkv = sb("wkv", [P, 2, 2 * D])
        bkv = sb("bkv", [P, 2 * D])
        wq = sb("wq", [P, 2, D])
        bqb = sb("bqb", [P, D])
        wa = sb("wa", [P, 2, D])
        bab = sb("bab", [P, D])
        skc = sb("skc", [P, 5])
        iota_n = sb("iota_n", [P, P])
        notlast = sb("notlast", [P, 1])
        notfirst = sb("notfirst", [P, 1])
        padi = sb("padi", [16, 2 * (TAIL // 16)], I32)

        thr = sb("thr", [P, 4])
        row1 = sb("row1", [1, P], I32)
        rowf = sb("rowf", [1, P])
        ones = sb("ones", [P, P])
        tcol = sb("tcol", [P, 16])
        rowi = sb("rowi", [P, 1], I32)
        lower = sb("lower", [P, P])
        diff = sb("diff", [P, P])
        iota_s = sb("iota_s", [P, SM])
        iota_c = sb("iota_c", [P, J])
        lastw = sb("lastw", [P, 1])
        act_a = sb("act_a", [P, SM])
        act_b = sb("act_b", [P, SM])
        nb_t = sb("nb_t", [P, SM])
        base_t = sb("base_t", [P, SM])
        nw_t = sb("nw_t", [P, SM])
        base_i = sb("base_i", [1, SM], I32)
        nb_i = sb("nb_i", [1, SM + 1], I32)
        cnt_i = sb("cnt_i", [1, 1], I32)

        xt = sb("xt", [P, 2, 2, D])
        xT = sb("xT", [P, 2, 512])
        kvs = sb("kvs", [P, 2, 2, 2 * D])

        dst_l = sb("dst_l", [P, 2, G + 2], I32)
        src_l = sb("src_l", [P, 2, G], I32)
        rel = sb("rel", [P, 2, G + 2])
        nbc = sb("nbc", [P, 2, 2])
        off_w = sb("off_w", [P, G])
        gidx = sb("gidx", [P, 2, G], I32)
        kv = sb("kv", [P, 2, G, 2 * D])
        onehot = sb("onehot", [P, 2, G, P])
        onehotT = sb("onehotT", [P, 2, G, P])
        assert RC <= G * P
        cmp = onehotT[:, 0].rearrange("p g k -> p (g k)")
        drow = onehotT[:, 1].rearrange("p g k -> p (g k)").bitcast(I32)[:, 0:RC]
        same = sb("same", [P, G + 1])
        msk = sb("msk", [P, G + 1])
        afwd = sb("afwd", [P, 2, H, G])
        headm = sb("headm", [P, 2, G])
        lk = sb("lk", [P, 4])
        mlc = sb("mlc", [P, 2, H])
        mlT = sb("mlT", [H, 2, 2, P])
        xw = sb("xw", [P, 2, D])
        xwT = sb("xwT", [P, D])
        qf = sb("qf", [P, 2, D])
        res = sb("res", [P, 2, D])
        prod = sb("prod", [P, 3, 2, D])
        score = sb("score", [P, H, G])
        fmax = sb("fmax", [P, H, G])
        xs = sb("xs", [H, P + 1])
        ut = sb("ut", [P, P])
        tu = sb("tu", [P, H, G])
        tl = sb("tl", [P, 2, H + 1, G])
        mc = sb("mc", [P, H])
        m4 = sb("m4", [P, 3, H])
        mrun = sb("mrun", [P, H])
        pres = sb("pres", [P, 1])
        dab = sb("dab", [P, 2, H])
        ab = sb("ab", [P, 2, H])
        dexp = sb("dexp", [P, G, H])
        state = sb("state", [P, H, DK + 1])
        part = sb("part", [P, H, DK + 1])
        cell = sb("cell", [P, 16])
        zz = sb("zz", [P, 2, H])
        tn = sb("tn", [P, D])
        tT = sb("tT", [P, D])
        yy = sb("yy", [P, D])
        scratch = sb("scratch", [P, D])
        eps_c = sb("eps_c", [P, 1])
        ln = sb("ln", [P, 9])
        outb = sb("outb", [P, 2, D])

        wts_in = sem("wts_in")
        row_in = sem("row_in")
        drow_in = sem("drow_in")
        pads_in = sem("pads_in")
        consts = sem("consts")
        idm = sem("idm")
        rz = sem("rz")
        pool_step = sem("pool_step")
        pad_tile = sem("pad_tile")
        dve_setup = sem("dve_setup")
        fold_in = sem("fold_in")
        fold_mm = sem("fold_mm")
        fold_cp = sem("fold_cp")
        skip_exp = sem("skip_exp")
        tab_mm = sem("tab_mm")
        tab_in = sem("tab_in")
        rows_idx = sem("rows_idx")
        tables = sem("tables")
        setup = sem("setup")
        x_in = [sem("x_in0"), sem("x_in1")]
        x_T = sem("x_T")
        x_Tc = sem("x_Tc")
        kv_mm = sem("kv_mm")
        kv_add = sem("kv_add")
        kv_out = [sem("kv_out0"), sem("kv_out1")]
        idx_in = sem("idx_in")
        xw_in = [sem("xw_in0"), sem("xw_in1")]
        e1_done = sem("e1_done")
        gat = [[sem(f"gat{b}_{q}") for q in range(NQ)] for b in range(2)]
        q_edge = sem("q_edge")
        q_used = sem("q_used")
        oh_ready = sem("oh_ready")
        oh_T = sem("oh_T")
        oh_Tc = sem("oh_Tc")
        mask_T = sem("mask_T")
        win_T = sem("win_T")
        win_Tc = sem("win_Tc")
        win_q = sem("win_q")
        q_done = sem("q_done")
        tail_ready = sem("tail_ready")
        tail_T = sem("tail_T")
        ut_ready = sem("ut_ready")
        carry_T = sem("carry_T")
        tl_ready = sem("tl_ready")
        nmax_mm = sem("nmax_mm")
        mc_ready = sem("mc_ready")
        maxe_mm = sem("maxe_mm")
        d_ready = sem("d_ready")
        ex_ready = sem("ex_ready")
        dab_ready = sem("dab_ready")
        ab_ready = sem("ab_ready")
        w_ready = sem("w_ready")
        agg_done = sem("agg_done")
        agg_read = sem("agg_read")
        tn_ready = sem("tn_ready")
        tn_T = sem("tn_T")
        tn_Tc = sem("tn_Tc")
        y_mm = sem("y_mm")
        yy_ready = sem("yy_ready")
        ln_step = sem("ln_step")
        rs_ready = sem("rs_ready")
        fin_done = sem("fin_done")
        out_done = sem("out_done")
        dstep = sem("dstep")

        def bc(ap, axis, n):
            shape = list(ap.shape)
            return ap.unsqueeze(axis).to_broadcast(shape[:axis] + [n] + shape[axis:])

        def turns(eng):
            eng.wait_ge(tables, 1)
            return eng.value_load(cnt_i[0:1, 0:1], min_val=1, max_val=SM // 2 - 1)

        N_WTS = 16 * (4 + 4 + HPB + 1 + 2 * HPB)
        N_CONST = 12

        def rows2(t, base):
            d = t.shape[1]
            return bass.AP(t.tensor, base, [[2 * d, P], [d, 2], [1, d]])

        def rows1(t, base):
            return bass.AP(t.tensor, base, [[t.shape[1], P], [1, t.shape[1]]])

        block = ctx.enter_context(nc.Block())

        @block.sync
        def _(sp):
            sp.dma_start(row1[0:1, 0:ROWS], bass.AP(dst.tensor, 0, [[RC, 1], [RC, ROWS]]),
                         allow_slow_non_contiguous=True).then_inc(row_in, 16)
            for k, wm in enumerate((Wk, Wv, Wq, Wa)):
                sp.dma_start(wl[:, k], wm.rearrange("(a p) i -> p a i", p=P)).then_inc(wts_in, 16)
            for k, bm in enumerate((bk, bv, bq, ba)):
                sp.dma_start(bcol[:, k], bm.rearrange("(a p) -> p a", p=P),
                             allow_slow_non_contiguous=True).then_inc(wts_in, 16)
            for q in range(HPB):
                sp.dma_start(pcol[DK * q:DK * q + DK, :],
                             bass.AP(rel_pri.tensor, q, [[0, DK], [HPB, 2]]),
                             allow_slow_non_contiguous=True).then_inc(wts_in, 16)
            sp.dma_start(skc[:, 0:1], bass.AP(skip.tensor, 0, [[0, P], [1, 1]])).then_inc(wts_in, 16)
            sp.wait_ge(rz, 1)
            for k, rm in enumerate((rel_att, rel_msg)):
                for q in range(HPB):
                    sp.dma_start(rfold[DK * q:DK * q + DK, k, :, DK * q:DK * q + DK],
                                 rm.rearrange("(a q) d e -> q d a e", q=HPB)[q]).then_inc(wts_in, 16)
            for k, (pad, arr) in enumerate(((dst_pad, dst), (src_pad, src))):
                sp.dma_start(pad[1:1 + E].rearrange("(a b) -> a b", a=16),
                             arr.rearrange("(a b) -> a b", a=16)).then_inc(pads_in, 16)
            sp.wait_ge(pad_tile, 2)
            for k, pad in enumerate((dst_pad, src_pad)):
                sp.dma_start(pad[0:1].rearrange("(a b) -> a b", a=1), padi[0:1, 0:1]).then_inc(pads_in, 16)
                sp.dma_start(pad[1 + E:EP].rearrange("(a b) -> a b", a=16),
                             padi[:, k * (TAIL // 16):(k + 1) * (TAIL // 16)]).then_inc(pads_in, 16)

            def load_tile(t, base):
                sp.wait_ge(x_T, t.done())
                sp.dma_start(xt[:, t.par], rows2(x, base)).then_inc(x_in[t.par], 16)

            def store_tile(t, base):
                sp.wait_ge(kv_add, t.done(credit=2))
                sp.dma_start(rows2(kv_dram, base), kvs[:, t.par]).then_inc(kv_out[t.par], 16)

            STEP = 2 * P * D
            load_tile(Chunk(0, 0), 0)
            with sp.Fori(0, PL - 1) as i:
                for b in range(2):
                    x_next = sp.snap(i * (2 * STEP) + (b + 1) * STEP)
                    kv_here = sp.snap(i * (4 * STEP) + b * 2 * STEP)
                    load_tile(Chunk(i, b + 1), x_next)
                    store_tile(Chunk(i, b), kv_here)
            load_tile(Chunk(PL - 1, 1), (2 * PL - 1) * STEP)
            store_tile(Chunk(PL - 1, 0), (2 * PL - 2) * 2 * STEP)
            load_tile(Chunk(PL, 0), (N - 2 * P) * D)
            store_tile(Chunk(PL - 1, 1), (2 * PL - 1) * 2 * STEP)
            sp.wait_ge(kv_out[1], 16 * (PL + 1))
            store_tile(Chunk(PL, 0), (N - 2 * P) * 2 * D)

            n = turns(sp)
            sp.wait_ge(pads_in, 96)

            def load_chunk(c, s):
                first = sp.value_load(base_i[0:1, bass.ds(s, 1)], min_val=0, max_val=EP - C - 2)
                second = sp.snap(first + 1)
                node = sp.value_load(nb_i[0:1, bass.ds(s + 1, 1)], min_val=0, max_val=(N - P) * D)
                sp.wait_ge(e1_done, c.done())
                sp.nop(nofuse=True)
                sp.dma_start(dst_l[:, c.par], bass.AP(dst_pad.tensor, first, [[G, P], [1, G + 2]]))\
                    .then_inc(idx_in, 16)
                sp.dma_start(src_l[:, c.par], bass.AP(src_pad.tensor, second, [[G, P], [1, G]]))\
                    .then_inc(idx_in, 16)
                sp.wait_ge(q_done, c.done())
                sp.nop(nofuse=True)
                sp.dma_start(xw[:, c.par], rows1(x, node)).then_inc(xw_in[c.par], 16)

            def store_window(c, s):
                node = sp.value_load(nb_i[0:1, bass.ds(s, 1)], min_val=0, max_val=(N - P) * D)
                sp.wait_ge(fin_done, c.done(credit=1))
                sp.nop(nofuse=True)
                sp.wait_ge(out_done, c.done(per=16, credit=32))
                sp.nop(nofuse=True)
                sp.dma_start(rows1(out, node), outb[:, c.par]).then_inc(out_done, 16)

            load_chunk(Chunk(0, 0), 0)
            with sp.Fori(0, n) as i:
                for b in range(2):
                    c = Chunk(i, b)
                    load_chunk(c.next(), 2 * i + b + 1)
                    store_window(c.prev(), 2 * i + b)
            store_window(Chunk(n, -1), 2 * n)
            sp.wait_ge(out_done, n * 32 + 48)
            sp.nop(nofuse=True)

        @block.gpsimd
        def _(pool):
            step = [0]

            def link(ins):
                step[0] += 1
                ins.then_inc(pool_step, 1)
                pool.wait_ge(pool_step, step[0])

            pool.memset(padi[:, 0:TAIL // 16], 1 << 20).then_inc(pad_tile, 1)
            pool.memset(padi[:, TAIL // 16:], 0).then_inc(pad_tile, 1)
            pool.memset(rfold[:, :, :, :], 0.0).then_inc(rz, 1)
            pool.memset(ones[:, :], 1.0).then_inc(consts, 1)
            link(pool.memset(ident[:, :], 0.0))
            pool.affine_select(out=ident[:, :], in_=ident[:, :], compare_op=ALU.not_equal, fill=1.0,
                               base=0, pattern=[[-1, P]], channel_multiplier=1).then_inc(consts, 1)
            pool.iota(thr[:, 0:1], pattern=[[0, 1]], base=0, channel_multiplier=P,
                      allow_small_or_imprecise_dtypes=True).then_inc(consts, 1)
            pool.iota(thr[:, 1:2], pattern=[[0, 1]], base=0, channel_multiplier=1,
                      allow_small_or_imprecise_dtypes=True).then_inc(consts, 1)
            pool.iota(iota_s[:, :], pattern=[[1, SM]], base=0, channel_multiplier=0,
                      allow_small_or_imprecise_dtypes=True).then_inc(consts, 1)
            pool.iota(iota_c[:, :], pattern=[[C, J]], base=C, channel_multiplier=0,
                      allow_small_or_imprecise_dtypes=True).then_inc(consts, 1)
            pool.iota(iota_n[:, :], pattern=[[1, P]], base=0, channel_multiplier=0,
                      allow_small_or_imprecise_dtypes=True).then_inc(consts, 1)
            link(pool.memset(lower[:, :], 1.0))
            pool.affine_select(out=lower[:, :], in_=lower[:, :], compare_op=ALU.is_gt, fill=0.0,
                               base=0, pattern=[[1, P]], channel_multiplier=-1).then_inc(consts, 1)
            link(pool.memset(diff[:, :], 0.0))
            link(pool.affine_select(out=diff[:, :], in_=diff[:, :], compare_op=ALU.not_equal, fill=1.0,
                                    base=-1, pattern=[[-1, P]], channel_multiplier=1))
            pool.affine_select(out=diff[:, :], in_=diff[:, :], compare_op=ALU.not_equal, fill=-1.0,
                               base=0, pattern=[[-1, P]], channel_multiplier=1).then_inc(consts, 1)
            link(pool.memset(lastw[:, :], 0.0))
            pool.affine_select(out=lastw[:, :], in_=lastw[:, :], compare_op=ALU.not_equal, fill=1e6,
                               base=1 - W, pattern=[[0, 1]], channel_multiplier=1).then_inc(consts, 1)
            link(pool.memset(notlast[:, :], 1.0))
            pool.affine_select(out=notlast[:, :], in_=notlast[:, :], compare_op=ALU.not_equal, fill=0.0,
                               base=1 - P, pattern=[[0, 1]], channel_multiplier=1).then_inc(consts, 1)
            link(pool.memset(notfirst[:, :], 0.0))
            pool.affine_select(out=notfirst[:, :], in_=notfirst[:, :], compare_op=ALU.not_equal, fill=-BIG,
                               base=0, pattern=[[0, 1]], channel_multiplier=1).then_inc(consts, 1)
            pool.wait_ge(rows_idx, 1)
            pool.indirect_dma_start(out=drow[:, :], out_offset=None,
                                    in_=dst.rearrange("(a b) -> a b", b=RC),
                                    in_offset=bass.IndirectOffsetOnAxis(ap=rowi[:, 0:1], axis=0),
                                    bounds_check=ROWS - 1, oob_is_err=False).then_inc(drow_in, 16)
            for b in range(2):
                pool.memset(kv[:, b], 0.0).then_inc(setup, 1)
            pool.wait_ge(kv_out[0], 16 * (PL + 2))
            pool.wait_ge(kv_out[1], 16 * (PL + 1))
            pool.wait_ge(setup, 2)
            n = turns(pool)
            last_row = pool.to_reg(N - 1)
            with pool.Fori(0, n) as i:
                for b in range(2):
                    c = Chunk(i, b)
                    pool.wait_ge(e1_done, c.done(credit=1))
                    pool.wait_ge(w_ready, c.done(per=NW))
                    pool.nop(nofuse=True)
                    for q, (g0, gn) in enumerate(PAIRS):
                        for g in range(g0, g0 + gn):
                            pool.indirect_dma_start(
                                out=kv[:, b, g, :], out_offset=None, in_=kv_dram,
                                in_offset=bass.IndirectOffsetOnAxis(ap=gidx[:, b, g:g + 1], axis=0),
                                bounds_check=last_row, oob_is_err=False).then_inc(gat[b][q], 16)

        @block.tensor
        def _(pe):
            pe.wait_ge(wts_in, N_WTS)
            pe.wait_ge(consts, N_CONST)
            pe.wait_ge(fold_in, 1)
            for k in range(4):
                for a in range(2):
                    r = rfold[:, k, a] if k < 3 else ident[:, :]
                    for kh in range(2):
                        nc.tensor.matmul(bank[2 * k][:, kh * D + a * P:kh * D + (a + 1) * P],
                                         wl[:, k, a, kh * P:(kh + 1) * P], r, start=True, stop=True)
                    last = nc.tensor.matmul(bank[2 * k + 1][:, a * P:(a + 1) * P], bwide[:, k, a], r,
                                            start=True, stop=True)
                last.then_inc(fold_mm, 1)
            pe.wait_ge(fold_cp, 4)
            pe.wait_ge(tab_in, 1)
            nc.tensor.matmul(bank[0][:, 0:ROWS], ones[0:1, :], rowf[0:1, 0:ROWS], start=True, stop=True)\
                .then_inc(tab_mm, 1)
            pe.wait_ge(tab_in, 2)
            nc.tensor.matmul(bank[1][:, 0:1], diff[:, :], tcol[:, 2:3], start=True, stop=True).then_inc(tab_mm, 1)
            pe.wait_ge(tab_in, 3)
            nc.tensor.matmul(bank[2][:, 0:1], lower[0:W, :], tcol[0:W, 4:5], start=True, stop=True)
            nc.tensor.matmul(bank[2][:, 1:2], ones[0:W, :], tcol[0:W, 4:5], start=True, stop=True)\
                .then_inc(tab_mm, 1)
            pe.wait_ge(tab_in, 4)
            nc.tensor.matmul(bank[3][:, 0:SM], cmp[0:W, 0:P], act_a[0:W, :], start=True, stop=True)
            nc.tensor.matmul(bank[4][:, 0:SM], cmp[0:W, P:2 * P], act_a[0:W, :], start=True, stop=True)\
                .then_inc(tab_mm, 1)

            def project(t):
                pe.wait_ge(x_in[t.par], t.landed())
                pe.wait_ge(x_Tc, t.done())
                for j in range(2):
                    for kh in range(2):
                        last = nc.tensor.transpose(bank[0][:, (2 * j + kh) * P:(2 * j + kh + 1) * P],
                                                   xt[:, t.par, j, kh * P:(kh + 1) * P], ident[:, :])
                last.then_inc(x_T, 1)
                pe.wait_ge(x_Tc, t.done(credit=1))
                pe.wait_ge(kv_add, t.done())
                for j in range(2):
                    for kh in range(2):
                        last = nc.tensor.matmul(bank[2 + 2 * t.par + j][:, :],
                                                xT[:, t.par, (2 * j + kh) * P:(2 * j + kh + 1) * P],
                                                wkv[:, kh], start=(kh == 0), stop=(kh == 1))
                last.then_inc(kv_mm, 1)

            pe.wait_ge(tables, 1)
            with pe.Fori(0, PL) as i:
                for b in range(2):
                    project(Chunk(i, b))
            project(Chunk(PL, 0))
            pe.wait_ge(kv_add, 2 * PL + 3)

            def window_q(c):
                pe.wait_ge(xw_in[c.par], c.landed())
                pe.wait_ge(q_done, c.done(credit=1))
                for kh in range(2):
                    last = nc.tensor.transpose(ps_win[:, kh * P:(kh + 1) * P], xw[:, c.par, kh * P:(kh + 1) * P],
                                               ident[:, :])
                last.then_inc(win_T, 1)
                pe.wait_ge(win_Tc, c.done())
                for kh in range(2):
                    last = nc.tensor.matmul(ps_win[:, D:2 * D], xwT[:, kh * P:(kh + 1) * P], wq[:, kh],
                                            start=(kh == 0), stop=(kh == 1))
                last.then_inc(win_q, 1)

            def spread_q(c, q):
                if q == 0:
                    pe.wait_ge(q_done, c.done(credit=2))
                    pe.wait_ge(oh_Tc, c.done(per=NT, credit=2))
                pe.wait_ge(q_used, c.done(per=NQ, credit=q + 1, back=NQ))
                g0, gn = PAIRS[q]
                for g in range(g0, g0 + gn):
                    last = nc.tensor.matmul(ps_q[(c.par + q) % 2][:, (g - g0) * D:(g - g0 + 1) * D],
                                            onehotT[:, c.par, g], qf[:, c.par], start=True, stop=True)
                last.then_inc(q_edge, 1)

            def transpose_onehots(c, t):
                g0, gn = TGROUPS[t]
                if t == 0:
                    pe.wait_ge(oh_ready, c.done())
                pe.wait_ge(oh_Tc, c.done(per=NT, credit=t + 1, back=NT))
                for g in range(g0, g0 + gn):
                    last = nc.tensor.transpose(ps_t[(c.par + t) % 2][:, (g - g0) * P:(g - g0 + 1) * P],
                                               onehot[:, c.par, g], ident[:, :])
                if t == NT - 1:
                    for m in range(2):
                        last = nc.tensor.transpose(ps_t[(c.par + t) % 2][0:H, (m + 2) * P:(m + 3) * P],
                                                   mlc[:, m], ident[:, :])
                last.then_inc(oh_T, 1)

            def finish_T(c):
                pe.wait_ge(tn_ready, c.done(credit=1))
                for kh in range(2):
                    last = nc.tensor.transpose(ps_fin[:, kh * P:(kh + 1) * P], tn[:, kh * P:(kh + 1) * P],
                                               ident[:, :])
                last.then_inc(tn_T, 1)

            def finish_mm(c):
                pe.wait_ge(tn_Tc, c.done(credit=1))
                for kh in range(2):
                    last = nc.tensor.matmul(ps_fin[:, D:2 * D], tT[:, kh * P:(kh + 1) * P], wa[:, kh],
                                            start=(kh == 0), stop=(kh == 1))
                last.then_inc(y_mm, 1)

            window_q(Chunk(0, 0))
            for t in range(NT):
                transpose_onehots(Chunk(0, 0), t)
            n = turns(pe)
            with pe.Fori(0, n) as i:
                for b in range(2):
                    c = Chunk(i, b)
                    for q in range(NQ):
                        spread_q(c, q)
                        if q == 4:
                            finish_T(c.prev())
                        if q == 5:
                            finish_mm(c.prev())
                    window_q(c.next())
                    pe.wait_ge(tail_ready, c.done())
                    nc.tensor.transpose(TAILT, fmax[:, :, G - 1], ident[:, :]).then_inc(tail_T, 1)
                    pe.wait_ge(ut_ready, c.done())
                    nc.tensor.transpose(CARRYT, ut[:, :], ident[:, :]).then_inc(carry_T, 1)
                    pe.wait_ge(tl_ready, c.done())
                    for g in range(G):
                        last = nc.tensor.matmul(NMAX, onehot[:, b, g], tl[:, b, :, g], start=(g == 0), stop=(g == G - 1))
                    last.then_inc(nmax_mm, 1)
                    pe.wait_ge(mc_ready, c.done())
                    for g in range(G):
                        last = nc.tensor.matmul(MAXE[:, g * H:(g + 1) * H], onehotT[:, b, g], mc[:, :],
                                                start=True, stop=True)
                    last.then_inc(maxe_mm, 1)
                    transpose_onehots(c.next(), 0)
                    transpose_onehots(c.next(), 1)
                    pe.wait_ge(agg_read, c.done())
                    for k, (g0, gn) in enumerate(WGROUPS):
                        pe.wait_ge(w_ready, c.done(per=NW, credit=NW + k + 1))
                        for g in range(g0, g0 + gn):
                            last = nc.tensor.matmul(ps_agg[:, 0:H * (DK + 1)], onehot[:, b, g],
                                                    wv[:, g].rearrange("p h d -> p (h d)"),
                                                    start=(g == 0), stop=(g == G - 1))
                        if k == len(WGROUPS) - 1:
                            last.then_inc(agg_done, 1)
                        if k + 2 < NT:
                            transpose_onehots(c.next(), k + 2)
            finish_T(Chunk(n, -1))
            finish_mm(Chunk(n, -1))

        @block.scalar
        def _(act):
            act.wait_ge(wts_in, N_WTS)
            nc.scalar.activation(skc[:, 1:2], skc[:, 0:1], ACT.Exp, scale=-1.0).then_inc(skip_exp, 1)

            def copy_xT(t):
                act.wait_ge(x_T, t.done(credit=2))
                act.wait_ge(kv_mm, t.done())
                nc.scalar.activation(xT[:, t.par], bank[0][:, :], ACT.Copy).then_inc(x_Tc, 1)

            with act.Fori(0, PL) as i:
                for b in range(2):
                    copy_xT(Chunk(i, b))
            copy_xT(Chunk(PL, 0))

            def copy_xwT(c):
                act.wait_ge(win_T, c.done())
                nc.scalar.activation(xwT[:, :], ps_win[:, 0:D], ACT.Copy).then_inc(win_Tc, 1)

            def copy_onehotT(c, t):
                g0, gn = TGROUPS[t]
                act.wait_ge(oh_T, c.done(per=NT, credit=t + 1, back=NT))
                src_bank = ps_t[(c.par + t) % 2]
                if t == NT - 1:
                    nc.scalar.activation(mlT[:, c.par].rearrange("p m k -> p (m k)"), src_bank[0:H, 2 * P:4 * P],
                                         ACT.Copy).then_inc(mask_T, 1)
                nc.scalar.activation(onehotT[:, c.par, g0:g0 + gn].rearrange("p g k -> p (g k)"),
                                     src_bank[:, 0:gn * P], ACT.Copy).then_inc(oh_Tc, 1)

            def copy_tT(c):
                act.wait_ge(tn_T, c.done(credit=1))
                nc.scalar.activation(tT[:, :], ps_fin[:, 0:D], ACT.Copy).then_inc(tn_Tc, 1)

            def statistics(c):
                act.wait_ge(yy_ready, c.done(credit=1))
                nc.scalar.activation(scratch[:, :], yy[:, :], ACT.Copy, accum_out=ln[:, 0:1]).then_inc(ln_step, 1)
                act.wait_ge(ln_step, c.done(per=4, credit=1))
                nc.scalar.activation(ln[:, 1:2], ln[:, 0:1], ACT.Copy, scale=-1.0 / D).then_inc(ln_step, 1)
                act.wait_ge(ln_step, c.done(per=4, credit=2))
                nc.scalar.activation(scratch[:, :], yy[:, :], ACT.Square, bias=ln[:, 1:2],
                                     accum_out=ln[:, 2:3]).then_inc(ln_step, 1)
                act.wait_ge(ln_step, c.done(per=4, credit=3))
                nc.scalar.activation(ln[:, 3:4], ln[:, 2:3], ACT.Ln, bias=eps_c[:, :], scale=1.0 / D)\
                    .then_inc(ln_step, 1)
                act.wait_ge(ln_step, c.done(per=4, credit=4))
                nc.scalar.activation(ln[:, 4:5], ln[:, 3:4], ACT.Exp, scale=-0.5).then_inc(rs_ready, 1)

            copy_xwT(Chunk(0, 0))
            for t in range(NT):
                copy_onehotT(Chunk(0, 0), t)
            n = turns(act)
            with act.Fori(0, n) as i:
                for b in range(2):
                    c = Chunk(i, b)
                    copy_tT(c.prev())
                    copy_xwT(c.next())
                    statistics(c.prev())
                    act.wait_ge(dab_ready, c.done())
                    act.wait_ge(agg_read, c.done())
                    nc.scalar.activation(ab[:, :, :], dab[:, :, :], ACT.Exp).then_inc(ab_ready, 1)
                    act.wait_ge(d_ready, c.done())
                    act.wait_ge(agg_done, c.done())
                    nc.scalar.activation(wv[:, :, :, DK], dexp[:, :, :], ACT.Exp).then_inc(ex_ready, 1)
                    for t in range(NT):
                        copy_onehotT(c.next(), t)
            copy_tT(Chunk(n, -1))
            statistics(Chunk(n, -1))

        @block.vector
        def _(v):
            step = [0]

            def link(ins):
                step[0] += 1
                ins.then_inc(dve_setup, 1)
                v.wait_ge(dve_setup, step[0])

            v.wait_ge(consts, N_CONST)
            v.wait_ge(wts_in, N_WTS)
            v.wait_ge(rz, 1)
            for k in range(4):
                for a in range(2):
                    link(v.tensor_copy(bwide[:, k, a], bcol[:, k, a:a + 1].to_broadcast([P, P])))
            for a in range(2):
                link(v.tensor_scalar(rfold[:, 2, a], ident[:, :], pcol[:, a:a + 1], 1.0 / math.sqrt(DK),
                                     ALU.mult, ALU.mult))
            link(v.memset(tl[:, :, :, :], 0.0))
            v.memset(xs[:, :], -BIG).then_inc(fold_in, 1)
            v.wait_ge(skip_exp, 1)
            link(v.tensor_scalar(skc[:, 2:3], skc[:, 1:2], 1.0, None, ALU.add))
            link(v.reciprocal(skc[:, 3:4], skc[:, 2:3]))
            link(v.tensor_scalar(skc[:, 4:5], skc[:, 3:4], -1.0, 2.0, ALU.mult, ALU.add))
            for k, (wt, off, bt) in enumerate(((wkv, 0, bkv), (wkv, D, bkv), (wq, 0, bqb), (wa, 0, bab))):
                v.wait_ge(fold_mm, k + 1)
                link(v.tensor_copy(wt[:, :, off:off + D], bank[2 * k][:, :].rearrange("p (a c) -> p a c", a=2)))
                if k < 3:
                    last = v.tensor_copy(bt[:, off:off + D], bank[2 * k + 1][:, 0:D])
                else:
                    last = v.tensor_scalar(bt[:, :], bank[2 * k + 1][:, 0:D], skc[:, 3:4], None, ALU.mult)
                last.then_inc(fold_cp, 1)
            v.wait_ge(row_in, 16)
            link(v.memset(rowf[:, :], 0.0))
            link(v.tensor_copy(rowf[0:1, 0:ROWS], row1[0:1, 0:ROWS]))
            link(v.tensor_scalar(tcol[:, 0:1], thr[:, 1:2], float(W), 1e6, ALU.is_ge, ALU.mult))
            link(v.tensor_scalar(tcol[:, 1:2], thr[:, 0:1], float(N - P), None, ALU.min))
            link(v.tensor_tensor(tcol[:, 0:1], tcol[:, 0:1], tcol[:, 1:2], ALU.add))
            v.memset(outb[:, :, :], 0.0).then_inc(tab_in, 1)
            v.wait_ge(tab_mm, 1)
            link(v.tensor_scalar(cmp[:, 0:ROWS], bank[0][:, 0:ROWS], tcol[:, 0:1], None, ALU.is_lt))
            link(v.tensor_reduce(tcol[:, 8:9], cmp[:, 0:ROWS], AX.X, ALU.add))
            link(v.tensor_scalar(tcol[:, 9:10], tcol[:, 8:9], -1.0, 0.0, ALU.add, ALU.max))
            v.tensor_copy(rowi[:, :], tcol[:, 9:10]).then_inc(rows_idx, 1)
            v.wait_ge(drow_in, 16)
            link(v.tensor_scalar(cmp[:, 0:RC], drow[:, :], tcol[:, 0:1], None, ALU.is_lt))
            link(v.tensor_reduce(tcol[:, 10:11], cmp[:, 0:RC], AX.X, ALU.add))
            v.scalar_tensor_tensor(out=tcol[:, 2:3], in0=tcol[:, 9:10], scalar=float(RC), in1=tcol[:, 10:11],
                                   op0=ALU.mult, op1=ALU.add).then_inc(tab_in, 1)
            v.wait_ge(tab_mm, 2)
            v.wait_ge(tab_in, 2)
            link(v.tensor_copy(tcol[:, 3:4], bank[1][:, 0:1]))
            link(v.tensor_scalar(cmp[:, 0:J], iota_c[:, :], tcol[:, 3:4], None, ALU.is_lt))
            link(v.tensor_reduce(tcol[:, 11:12], cmp[:, 0:J], AX.X, ALU.add))
            v.tensor_scalar(tcol[:, 4:5], tcol[:, 11:12], 1.0, None, ALU.add).then_inc(tab_in, 1)
            v.wait_ge(tab_mm, 3)
            v.wait_ge(tab_in, 3)
            link(v.tensor_copy(tcol[:, 5:6], bank[2][:, 0:1]))
            link(v.tensor_tensor(tcol[:, 12:13], tcol[:, 5:6], tcol[:, 4:5], ALU.add))
            link(v.tensor_tensor(tcol[:, 6:7], tcol[:, 12:13], lastw[:, :], ALU.add))
            link(v.tensor_scalar(act_b[:, :], iota_s[:, :], tcol[:, 6:7], None, ALU.is_ge))
            link(v.scalar_tensor_tensor(out=act_a[:, :], in0=iota_s[:, :], scalar=tcol[:, 5:6], in1=act_b[:, :],
                                        op0=ALU.is_ge, op1=ALU.subtract))
            link(v.scalar_tensor_tensor(out=tcol[:, 7:8], in0=tcol[:, 5:6], scalar=-float(C), in1=tcol[:, 2:3],
                                        op0=ALU.mult, op1=ALU.add))
            link(v.tensor_scalar(cmp[:, 0:P], ones[:, :], tcol[:, 0:1], None, ALU.mult))
            link(v.tensor_scalar(cmp[:, P:2 * P], ones[:, :], tcol[:, 7:8], None, ALU.mult))
            link(v.tensor_copy(tcol[:, 13:14], bank[2][:, 1:2]))
            link(v.tensor_scalar(act_b[:, 0:SM // 2], iota_s[:, 0:SM // 2], 2.0, tcol[:, 13:14], ALU.mult,
                                 ALU.is_lt))
            link(v.tensor_reduce(tcol[:, 14:15], act_b[:, 0:SM // 2], AX.X, ALU.add))
            link(v.tensor_copy(cnt_i[0:1, 0:1], tcol[0:1, 14:15]))
            v.memset(yy[:, :], 0.0).then_inc(tab_in, 1)
            v.wait_ge(tab_mm, 4)
            link(v.tensor_copy(nb_t[:, :], bank[3][:, 0:SM]))
            link(v.scalar_tensor_tensor(out=base_t[:, :], in0=iota_s[:, :], scalar=float(C), in1=bank[4][:, 0:SM],
                                        op0=ALU.mult, op1=ALU.add))
            link(v.tensor_copy(base_i[0:1, :], base_t[0:1, :]))
            link(v.memset(nb_i[0:1, 0:1], 0))
            link(v.tensor_scalar(nb_i[0:1, 1:SM + 1], nb_t[0:1, :], float(D), None, ALU.mult))
            link(v.memset(nw_t[:, :], -BIG))
            link(v.tensor_tensor(nw_t[:, 1:SM], nb_t[:, 1:SM], nb_t[:, 0:SM - 1], ALU.is_equal))
            link(v.tensor_scalar(nw_t[:, 1:SM], nw_t[:, 1:SM], BIG, -BIG, ALU.mult, ALU.add))
            link(v.memset(afwd[:, :, :, 0:1], -BIG))
            link(v.memset(ut[:, :], 0.0))
            link(v.memset(eps_c[:, :], EPS))
            link(v.memset(mrun[:, :], -BIG))
            link(v.memset(state[:, :, :], 0.0))
            link(v.memset(ab[:, :, :], 0.0))
            link(v.memset(res[:, :, :], 0.0))
            link(v.memset(ps_agg[:, :], 0.0))
            for k, (s, by) in enumerate(((x_T, 2), (x_Tc, 1), (kv_mm, 2), (kv_out[0], 16), (kv_out[1], 16),
                          (kv_add, 2), (e1_done, 1), (q_done, 2), (out_done, 32), (w_ready, 2 * NW), (q_used, 2),
                          (oh_Tc, 2), (agg_done, 1), (ab_ready, 1))):
                v.memset(cell[:, k:k + 1], 0.0).then_inc(s, by)
            v.memset(cell[:, 15:16], 0.0).then_inc(tables, 1)

            def add_bias(t):
                v.wait_ge(kv_mm, t.done(credit=2))
                v.wait_ge(kv_out[t.par], t.landed())
                for j in range(2):
                    last = v.tensor_tensor(kvs[:, t.par, j], bank[2 + 2 * t.par + j][:, :], bkv[:, :], ALU.add)
                last.then_inc(kv_add, 1)

            with v.Fori(0, PL) as i:
                for b in range(2):
                    add_bias(Chunk(i, b))
            add_bias(Chunk(PL, 0))

            def lapped(ins):
                count[0] += 1
                ins.then_inc(dstep, 1)
                return count[0]

            def settle(c, k):
                v.wait_ge(dstep, c.done(per=K_DVE, credit=STEPS0 + k, back=K_DVE))

            def dlink(c, ins):
                settle(c, lapped(ins))

            def edges_in(c, at):
                p = c.par
                v.wait_ge(idx_in, c.done(per=32))
                lapped(v.tensor_copy(nbc[:, p, 0:1], nb_t[:, bass.ds(c.number(), 1)]))
                dlink(at, v.tensor_copy(nbc[:, p, 1:2], nw_t[:, bass.ds(c.number(), 1)]))
                dlink(at, v.tensor_scalar(rel[:, p], dst_l[:, p], nbc[:, p, 0:1], None, ALU.subtract))
                dlink(at, v.tensor_scalar(off_w[:, :], rel[:, p, 1:G + 1], float(P), FAR, ALU.is_ge, ALU.mult))
                v.tensor_tensor(gidx[:, p], off_w[:, :], src_l[:, p], ALU.add).then_inc(e1_done, 1)

            def one_hots(c, at):
                lapped(v.tensor_tensor(onehot[:, c.par], bc(iota_n[:, :], 1, G), bc(rel[:, c.par, 1:G + 1], 2, P),
                                       ALU.is_equal))

            def masks(c, at):
                p = c.par
                dlink(at, v.tensor_tensor(same[:, :], rel[:, p, 1:G + 2], rel[:, p, 0:G + 1], ALU.is_equal))
                dlink(at, v.tensor_tensor(same[:, G:G + 1], same[:, G:G + 1], notlast[:, :], ALU.mult))
                dlink(at, v.tensor_scalar(msk[:, :], same[:, :], BIG, -BIG, ALU.mult, ALU.add))
                lapped(v.tensor_scalar(tl[:, p, H, :], same[:, 1:G + 1], -1.0, 1.0, ALU.mult, ALU.add))
                lapped(v.tensor_copy(afwd[:, p, :, 1:G], bc(msk[:, 1:G], 1, H)))
                lapped(v.tensor_tensor(lk[:, 0:1], msk[:, 0:1], notfirst[:, :], ALU.min))
                dlink(at, v.tensor_reduce(lk[:, 1:2], msk[:, 1:G], AX.X, ALU.min))
                dlink(at, v.tensor_tensor(lk[:, 2:3], lk[:, 0:1], lk[:, 1:2], ALU.add))
                lapped(v.tensor_copy(mlc[:, 1], lk[:, 0:1].to_broadcast([P, H])))
                lapped(v.tensor_copy(mlc[:, 0], lk[:, 2:3].to_broadcast([P, H])))
                dlink(at, v.tensor_scalar(headm[:, p], rel[:, p, 1:G + 1], rel[:, p, 1:2], BIG, ALU.is_equal, ALU.mult))
                v.tensor_scalar(headm[:, p], headm[:, p], -BIG, None, ALU.add).then_inc(oh_ready, 1)

            def window_in(c):
                v.wait_ge(win_q, c.done())
                v.tensor_tensor(qf[:, c.par], ps_win[:, D:2 * D], bqb[:, :], ALU.add)
                v.scalar_tensor_tensor(out=res[:, c.par], in0=xw[:, c.par], scalar=skc[:, 4:5], in1=bab[:, :],
                                       op0=ALU.mult, op1=ALU.add).then_inc(q_done, 1)

            def multiply(c, q):
                g0, gn = PAIRS[q]
                v.wait_ge(gat[c.par][q], c.landed(per=16 * gn))
                v.wait_ge(q_edge, c.done(per=NQ, credit=q + 1, back=NQ))
                v.tensor_tensor(prod[:, q % 3, 0:gn], kv[:, c.par, g0:g0 + gn, 0:D],
                                ps_q[(c.par + q) % 2][:, 0:gn * D].rearrange("p (g d) -> p g d", d=D),
                                ALU.mult).then_inc(q_used, 1)

            def scores(c, q):
                g0, gn = PAIRS[q]
                v.wait_ge(q_used, c.done(per=NQ, credit=2 + q + 1, back=NQ))
                return lapped(v.tensor_reduce(score[:, :, g0:g0 + gn].rearrange("p h g -> p g h"),
                                              prod[:, q % 3, 0:gn].rearrange("p g (h d) -> p g h d", d=DK),
                                              AX.X, ALU.add))

            def merge(c, at):
                v.wait_ge(agg_done, c.done(credit=1))
                v.wait_ge(ab_ready, c.done(credit=1))
                v.tensor_tensor(part[:, :, :], ps_agg[:, 0:H * (DK + 1)].rearrange("p (h d) -> p h d", h=H),
                                bc(ab[:, 1], 2, DK + 1), ALU.mult)
                v.tensor_tensor(state[:, :, :], state[:, :, :], bc(ab[:, 0], 2, DK + 1), ALU.mult).then_inc(agg_read, 1)
                v.wait_ge(agg_read, c.done(credit=1))
                dlink(at, v.tensor_tensor(state[:, :, :], state[:, :, :], part[:, :, :], ALU.add))
                dlink(at, v.scalar_tensor_tensor(out=zz[:, 0], in0=state[:, :, DK], scalar=0.0, in1=state[:, :, DK],
                                                 op0=ALU.is_equal, op1=ALU.add))
                dlink(at, v.reciprocal(zz[:, 1], zz[:, 0]))
                v.tensor_tensor(tn[:, :].rearrange("p (h d) -> p h d", h=H), state[:, :, 0:DK],
                                bc(zz[:, 1], 2, DK), ALU.mult).then_inc(tn_ready, 1)

            def finish(c, at):
                v.wait_ge(y_mm, c.done(credit=1))
                v.wait_ge(out_done, c.done(per=16, credit=16))
                v.scalar_tensor_tensor(out=yy[:, :], in0=ps_fin[:, D:2 * D], scalar=skc[:, 3:4],
                                       in1=res[:, c.par], op0=ALU.mult, op1=ALU.add).then_inc(yy_ready, 1)

            def normalise(c, at):
                v.wait_ge(rs_ready, c.done(credit=1))
                lapped(v.tensor_scalar(ln[:, 5:6], ln[:, 2:3], 1.0 / D, EPS, ALU.mult, ALU.add))
                dlink(at, v.tensor_tensor(ln[:, 6:7], ln[:, 4:5], ln[:, 4:5], ALU.mult))
                dlink(at, v.scalar_tensor_tensor(out=ln[:, 7:8], in0=ln[:, 6:7], scalar=-0.5, in1=ln[:, 5:6],
                                                 op0=ALU.mult, op1=ALU.mult))
                dlink(at, v.scalar_tensor_tensor(out=ln[:, 8:9], in0=ln[:, 7:8], scalar=1.5, in1=ln[:, 4:5],
                                                 op0=ALU.add, op1=ALU.mult))
                v.tensor_scalar(outb[:, c.par], yy[:, :], ln[:, 1:2], ln[:, 8:9], ALU.add, ALU.mult)\
                    .then_inc(fin_done, 1)

            def flat(t):
                return t.rearrange("p h g -> p (h g)")

            count = [0]
            K_DVE, STEPS0 = 0, 0
            c0 = Chunk(0, 0)
            edges_in(c0, c0)
            one_hots(c0, c0)
            masks(c0, c0)
            window_in(c0)
            K_DVE, STEPS0 = 38, count[0]
            n = turns(v)
            with v.Fori(0, n) as i:
                for b in range(2):
                    c = Chunk(i, b)
                    count[0] = 0
                    edges_in(c.next(), c)
                    multiply(c, 0)
                    reduced = []
                    for q in range(1, NQ):
                        if q >= 3:
                            settle(c, reduced[q - 3])
                        multiply(c, q)
                        reduced.append(scores(c, q - 1))
                        if q == 2:
                            merge(c.prev(), c)
                        if q == 5:
                            finish(c.prev(), c)
                        if q == 7:
                            normalise(c.prev(), c)
                    settle(c, scores(c, NQ - 1))
                    v.tensor_tensor_scan(flat(fmax[:, :, :]), flat(afwd[:, b]), flat(score[:, :, :]), -BIG,
                                         ALU.add, ALU.max).then_inc(tail_ready, 1)
                    one_hots(c.next(), c)
                    v.wait_ge(tail_T, c.done())
                    v.wait_ge(mask_T, c.done())
                    dlink(c, v.tensor_tensor_scan(xs[:, 1:P + 1], mlT[:, b, 0], TAILT, -BIG, ALU.add, ALU.max))
                    v.tensor_tensor(ut[0:H, :], xs[:, 0:P], mlT[:, b, 1], ALU.add).then_inc(ut_ready, 1)
                    masks(c.next(), c)
                    v.wait_ge(carry_T, c.done())
                    v.wait_ge(tail_ready, c.done())
                    dlink(c, v.tensor_tensor(tu[:, :, :], bc(CARRY, 2, G), bc(headm[:, b], 1, H), ALU.add))
                    dlink(c, v.tensor_tensor(tu[:, :, :], tu[:, :, :], fmax[:, :, :], ALU.max))
                    v.tensor_tensor(tl[:, b, 0:H], tu[:, :, :], bc(tl[:, b, H], 1, H), ALU.mult)\
                        .then_inc(tl_ready, 1)
                    window_in(c.next())
                    v.wait_ge(nmax_mm, c.done())
                    v.tensor_scalar(pres[:, :], NMAX[:, H:H + 1], BIG, -BIG, ALU.mult, ALU.add)
                    v.tensor_copy(mc[:, :], NMAX[:, 0:H]).then_inc(mc_ready, 1)
                    v.wait_ge(mc_ready, c.done())
                    lapped(v.tensor_scalar(m4[:, 0], mc[:, :], pres[:, :], None, ALU.add))
                    dlink(c, v.tensor_scalar(m4[:, 1], mrun[:, :], nbc[:, b, 1:2], None, ALU.add))
                    dlink(c, v.tensor_tensor(mrun[:, :], m4[:, 0], m4[:, 1], ALU.max))
                    v.tensor_tensor(dab[:, 0], m4[:, 1], mrun[:, :], ALU.subtract)
                    v.tensor_tensor(dab[:, 1], m4[:, 0], mrun[:, :], ALU.subtract).then_inc(dab_ready, 1)
                    v.wait_ge(maxe_mm, c.done())
                    v.tensor_tensor(dexp[:, :, :], score[:, :, :].rearrange("p h g -> p g h"),
                                    MAXE.rearrange("p (g h) -> p g h", h=H), ALU.subtract).then_inc(d_ready, 1)
                    v.wait_ge(ex_ready, c.done())
                    for g0, gn in WGROUPS:
                        v.tensor_tensor(wv[:, g0:g0 + gn, :, 0:DK],
                                        kv[:, b, g0:g0 + gn, D:2 * D].rearrange("p g (h d) -> p g h d", d=DK),
                                        bc(wv[:, g0:g0 + gn, :, DK], 3, DK), ALU.mult).then_inc(w_ready, 1)
                    assert count[0] == K_DVE, count
            end = Chunk(n, -1)
            at = Chunk(n, 0)
            count[0] = 0
            merge(end, at)
            finish(end, at)
            normalise(end, at)


NAMES = ["x", "src", "dst", "L0_gnn_Wk", "L0_gnn_bk", "L0_gnn_Wq", "L0_gnn_bq", "L0_gnn_Wv", "L0_gnn_bv",
         "L0_gnn_Wa", "L0_gnn_ba", "L0_gnn_rel_att", "L0_gnn_rel_msg", "L0_gnn_rel_pri", "L0_gnn_skip"]


def kernel(**inputs):
    import numpy as np
    import concourse.bacc as bacc
    from concourse.bass_utils import run_bass_kernel_spmd

    nc = bacc.Bacc("TRN2", target_bir_lowering=False, num_devices=1)
    arrays, args = {}, []
    for name in NAMES:
        a = np.ascontiguousarray(inputs[name])
        a = a.reshape(1) if a.ndim == 0 else a
        arrays[name] = a
        args.append(nc.dram_tensor(name, a.shape, mybir.dt.from_np(a.dtype), kind="ExternalInput").ap())
    out = nc.dram_tensor("result", arrays["x"].shape, F32, kind="ExternalOutput").ap()
    gnn_program(nc, *args, out)
    return run_bass_kernel_spmd(nc, [arrays], core_ids=[0]).results[0]["result"]
```

```python
from contextlib import ExitStack
import math

import concourse.bass as bass
from concourse import mybir

ALU = mybir.AluOpType
ACT = mybir.ActivationFunctionType
AX = mybir.AxisListType
F32 = mybir.dt.float32
I32 = mybir.dt.int32

P = 128
G = 17
C = P * G
BIG = 1e30
FAR = float(1 << 22)
EPS = 1e-5
PAIRS = [(g, min(2, G - g)) for g in range(0, G, 2)]
NQ = len(PAIRS)
TGROUPS = [(g, min(4, G - g)) for g in range(0, G, 4)]
NT = len(TGROUPS)


class Chunk:

    def __init__(self, turn, off):
        self.turn, self.off, self.par = turn, off, off % 2

    def done(self, per=1, credit=0, back=0):
        return self.turn * (2 * per) + ((self.off + 1) * per + credit - back)

    def landed(self, per=16):
        return self.turn * per + (self.off // 2 + 1) * per

    def number(self):
        return self.turn * 2 + self.off

    def next(self):
        return Chunk(self.turn, self.off + 1)

    def prev(self):
        return Chunk(self.turn, self.off - 1)


def gnn_program(nc, x, src, dst, Wk, bk, Wq, bq, Wv, bv, Wa, ba, rel_att, rel_msg, rel_pri, skip, out):
    N, D = x.shape
    E = src.shape[0]
    H, DK, _ = rel_att.shape
    HPB = P // DK
    assert D == 2 * P and H * DK == D and H == 8
    W = -(-N // P)
    ROWS = 125
    RC = E // ROWS
    assert ROWS * RC == E and W + 1 <= P
    J = E // C + 1
    SM = 2 * ((W + J + 6) // 2)
    WC = H * (DK + 1)
    WX = WC + H + 1
    assert SM <= 512
    TAIL = 16 * (-(-(4 * C + 16) // 16))
    EP = 1 + E + TAIL
    NPAIR = -(-N // (2 * P))
    PL = NPAIR // 2
    assert NPAIR == 2 * PL + 1

    with ExitStack() as ctx:
        def sb(name, shape, dt=F32):
            return ctx.enter_context(nc.sbuf_tensor(name, shape, dt))

        def sem(name):
            return ctx.enter_context(nc.semaphore(name))

        kv_dram = nc.dram_tensor("kv_rows", (N, 2 * D), F32, kind="Internal").ap()
        src_pad = nc.dram_tensor("src_pad", (EP,), I32, kind="Internal").ap()
        dst_pad = nc.dram_tensor("dst_pad", (EP,), I32, kind="Internal").ap()

        bank = [ctx.enter_context(nc.psum_tensor(f"bank{i}", [P, 512], F32)) for i in range(8)]
        ps_t = bank[0:2]
        ps_q = bank[2:4]
        ps_agg = bank[4]
        ps_small = bank[5]
        ps_fin = bank[6]
        ps_win = bank[7]
        TAILT = ps_small[0:H, 0:P]
        HEADT = ps_small[0:H, P:2 * P]
        CARRYT = [ps_small[:, (k + 2) * P:(k + 3) * P] for k in range(2)]
        NMAX = ps_agg[:, WC:WX]

        ident = sb("ident", [P, P])
        wv = sb("wv", [P, G, WX])
        wl = bass.AP(wv, 0, [[G * WX, P], [2 * D, 4], [D, 2], [1, D]])
        rfold = sb("rfold", [P, 3, 2, P])
        bcol = sb("bcol", [P, 4, 2])
        bwide = sb("bwide", [P, 4, 2, P])
        pcol = sb("pcol", [P, 2])
        wkv = sb("wkv", [P, 2, 2 * D])
        bkv = sb("bkv", [P, 2 * D])
        wq = sb("wq", [P, 2, D])
        bqb = sb("bqb", [P, D])
        wa = sb("wa", [P, 2, D])
        bab = sb("bab", [P, D])
        skc = sb("skc", [P, 5])
        iota_n = sb("iota_n", [P, P])
        notlast = sb("notlast", [P, 1])
        notfirst = sb("notfirst", [P, 1])
        padi = sb("padi", [16, 2 * (TAIL // 16)], I32)

        thr = sb("thr", [P, 4])
        row1 = sb("row1", [1, P], I32)
        rowf = sb("rowf", [1, P])
        ones = sb("ones", [P, P])
        tcol = sb("tcol", [P, 16])
        rowi = sb("rowi", [P, 1], I32)
        lower = sb("lower", [P, P])
        diff = sb("diff", [P, P])
        iota_s = sb("iota_s", [P, SM])
        iota_c = sb("iota_c", [P, J])
        lastw = sb("lastw", [P, 1])
        act_a = sb("act_a", [P, SM])
        act_b = sb("act_b", [P, SM])
        nb_t = sb("nb_t", [P, SM])
        base_t = sb("base_t", [P, SM])
        nw_t = sb("nw_t", [P, SM])
        base_i = sb("base_i", [1, SM], I32)
        nb_i = sb("nb_i", [1, SM + 1], I32)
        cnt_i = sb("cnt_i", [1, 1], I32)

        xt = sb("xt", [P, 2, 2, D])
        xT = sb("xT", [P, 2, 512])
        kvs = sb("kvs", [P, 2, 2, 2 * D])

        dst_l = sb("dst_l", [P, 2, G + 2], I32)
        src_l = sb("src_l", [P, 2, G], I32)
        rel = sb("rel", [P, 2, G + 2])
        nbc = sb("nbc", [P, 1])
        nwc = sb("nwc", [P, 2])
        off_w = sb("off_w", [P, G])
        gidx = sb("gidx", [P, 2, G], I32)
        kv = sb("kv", [P, 2, G, 2 * D])
        onehot = sb("onehot", [P, 2, G, P])
        onehotT = sb("onehotT", [P, 2, G, P])
        assert RC <= G * P
        cmp = onehotT[:, 0].rearrange("p g k -> p (g k)")
        drow = onehotT[:, 1].rearrange("p g k -> p (g k)").bitcast(I32)[:, 0:RC]
        same = sb("same", [P, G + 1])
        msk = sb("msk", [P, G + 1])
        runs = sb("runs", [P, 2, H * G + 1])
        headm = sb("headm", [P, 2, 2, G])
        lastedge = sb("lastedge", [P, 2, G])
        lk = sb("lk", [P, 4])
        mlc = sb("mlc", [P, 2, H])
        mlT = sb("mlT", [H, 2, 1, P])
        linkT = sb("linkT", [H, 2, P + 1])
        passT = sb("passT", [H, 2, P])
        xw = sb("xw", [P, 2, D])
        xwT = sb("xwT", [P, D])
        qf = sb("qf", [P, 2, D])
        res = sb("res", [P, 2, D])
        prod = sb("prod", [P, 3, 2, D])
        score = sb("score", [P, H, G])
        fmax = sb("fmax", [P, H, G])
        xs = sb("xs", [H, P + 1])
        ys = sb("ys", [H, P + 1])
        ut = sb("ut", [P, 2, P])
        bmax = sb("bmax", [P, H, G])
        tu = sb("tu", [P, 2, H, G])
        m4 = sb("m4", [P, 3, H])
        mrun = sb("mrun", [P, H])
        pres = sb("pres", [P, 1])
        dab = sb("dab", [P, 2, H])
        ab = sb("ab", [P, 2, H])
        dexp = sb("dexp", [P, G, H])
        state = sb("state", [P, H, DK + 1])
        part = sb("part", [P, H, DK + 1])
        cell = sb("cell", [P, 16])
        zz = sb("zz", [P, 2, H])
        tn = sb("tn", [P, D])
        tT = sb("tT", [P, D])
        yy = sb("yy", [P, D])
        scratch = sb("scratch", [P, D])
        eps_c = sb("eps_c", [P, 1])
        ln = sb("ln", [P, 9])
        outb = sb("outb", [P, 2, D])

        wts_in = sem("wts_in")
        row_in = sem("row_in")
        drow_in = sem("drow_in")
        pads_in = sem("pads_in")
        consts = sem("consts")
        idm = sem("idm")
        rz = sem("rz")
        pool_step = sem("pool_step")
        pad_tile = sem("pad_tile")
        dve_setup = sem("dve_setup")
        fold_in = sem("fold_in")
        fold_mm = sem("fold_mm")
        fold_cp = sem("fold_cp")
        skip_exp = sem("skip_exp")
        tab_mm = sem("tab_mm")
        tab_in = sem("tab_in")
        rows_idx = sem("rows_idx")
        tables = sem("tables")
        setup = sem("setup")
        x_in = [sem("x_in0"), sem("x_in1")]
        x_T = sem("x_T")
        x_Tc = sem("x_Tc")
        kv_mm = sem("kv_mm")
        kv_add = sem("kv_add")
        kv_out = [sem("kv_out0"), sem("kv_out1")]
        idx_in = sem("idx_in")
        xw_in = [sem("xw_in0"), sem("xw_in1")]
        e1_done = sem("e1_done")
        gat = [[sem(f"gat{b}_{q}") for q in range(NQ)] for b in range(2)]
        q_edge = sem("q_edge")
        q_used = sem("q_used")
        oh_ready = sem("oh_ready")
        oh_T = sem("oh_T")
        oh_Tc = sem("oh_Tc")
        mask_T = sem("mask_T")
        win_T = sem("win_T")
        win_Tc = sem("win_Tc")
        win_q = sem("win_q")
        q_done = sem("q_done")
        res_done = sem("res_done")
        masks_ready = sem("masks_ready")
        tail_ready = sem("tail_ready")
        tail_T = sem("tail_T")
        ut_ready = sem("ut_ready")
        carry_T = sem("carry_T")
        d_ready = sem("d_ready")
        ex_ready = sem("ex_ready")
        dab_ready = sem("dab_ready")
        ab_ready = sem("ab_ready")
        w_ready = sem("w_ready")
        agg_done = sem("agg_done")
        agg_read = sem("agg_read")
        tn_ready = sem("tn_ready")
        tn_T = sem("tn_T")
        tn_Tc = sem("tn_Tc")
        y_mm = sem("y_mm")
        yy_ready = sem("yy_ready")
        ln_step = sem("ln_step")
        rs_ready = sem("rs_ready")
        fin_done = sem("fin_done")
        out_done = sem("out_done")
        dstep = sem("dstep")

        def bc(ap, axis, n):
            shape = list(ap.shape)
            return ap.unsqueeze(axis).to_broadcast(shape[:axis] + [n] + shape[axis:])

        def heads(ap):
            dims = " ".join("abc"[:len(ap.shape) - 1])
            return ap.rearrange(f"{dims} (h d) -> {dims} h d", h=H)

        def turns(eng):
            eng.wait_ge(tables, 1)
            return eng.value_load(cnt_i[0:1, 0:1], min_val=1, max_val=SM // 2 - 1)

        N_WTS = 16 * (4 + 4 + HPB + 1 + 2 * HPB)
        N_CONST = 12

        def rows2(t, base):
            d = t.shape[1]
            return bass.AP(t.tensor, base, [[2 * d, P], [d, 2], [1, d]])

        def rows1(t, base):
            return bass.AP(t.tensor, base, [[t.shape[1], P], [1, t.shape[1]]])

        block = ctx.enter_context(nc.Block())

        @block.sync
        def _(sp):
            sp.dma_start(row1[0:1, 0:ROWS], bass.AP(dst.tensor, 0, [[RC, 1], [RC, ROWS]]),
                         allow_slow_non_contiguous=True).then_inc(row_in, 16)
            for k, wm in enumerate((Wk, Wv, Wq, Wa)):
                sp.dma_start(wl[:, k], wm.rearrange("(a p) i -> p a i", p=P)).then_inc(wts_in, 16)
            for k, bm in enumerate((bk, bv, bq, ba)):
                sp.dma_start(bcol[:, k], bm.rearrange("(a p) -> p a", p=P),
                             allow_slow_non_contiguous=True).then_inc(wts_in, 16)
            for q in range(HPB):
                sp.dma_start(pcol[DK * q:DK * q + DK, :],
                             bass.AP(rel_pri.tensor, q, [[0, DK], [HPB, 2]]),
                             allow_slow_non_contiguous=True).then_inc(wts_in, 16)
            sp.dma_start(skc[:, 0:1], bass.AP(skip.tensor, 0, [[0, P], [1, 1]])).then_inc(wts_in, 16)
            sp.wait_ge(rz, 1)
            for k, rm in enumerate((rel_att, rel_msg)):
                for q in range(HPB):
                    sp.dma_start(rfold[DK * q:DK * q + DK, k, :, DK * q:DK * q + DK],
                                 rm.rearrange("(a q) d e -> q d a e", q=HPB)[q]).then_inc(wts_in, 16)
            for k, (pad, arr) in enumerate(((dst_pad, dst), (src_pad, src))):
                sp.dma_start(pad[1:1 + E].rearrange("(a b) -> a b", a=16),
                             arr.rearrange("(a b) -> a b", a=16)).then_inc(pads_in, 16)
            sp.wait_ge(pad_tile, 2)
            for k, pad in enumerate((dst_pad, src_pad)):
                sp.dma_start(pad[0:1].rearrange("(a b) -> a b", a=1), padi[0:1, 0:1]).then_inc(pads_in, 16)
                sp.dma_start(pad[1 + E:EP].rearrange("(a b) -> a b", a=16),
                             padi[:, k * (TAIL // 16):(k + 1) * (TAIL // 16)]).then_inc(pads_in, 16)

            def load_tile(t, base):
                sp.wait_ge(x_T, t.done())
                sp.dma_start(xt[:, t.par], rows2(x, base)).then_inc(x_in[t.par], 16)

            def store_tile(t, base):
                sp.wait_ge(kv_add, t.done(credit=2))
                sp.dma_start(rows2(kv_dram, base), kvs[:, t.par]).then_inc(kv_out[t.par], 16)

            STEP = 2 * P * D
            load_tile(Chunk(0, 0), 0)
            with sp.Fori(0, PL - 1) as i:
                for b in range(2):
                    x_next = sp.snap(i * (2 * STEP) + (b + 1) * STEP)
                    kv_here = sp.snap(i * (4 * STEP) + b * 2 * STEP)
                    load_tile(Chunk(i, b + 1), x_next)
                    store_tile(Chunk(i, b), kv_here)
            load_tile(Chunk(PL - 1, 1), (2 * PL - 1) * STEP)
            store_tile(Chunk(PL - 1, 0), (2 * PL - 2) * 2 * STEP)
            load_tile(Chunk(PL, 0), (N - 2 * P) * D)
            store_tile(Chunk(PL - 1, 1), (2 * PL - 1) * 2 * STEP)
            sp.wait_ge(kv_out[1], 16 * (PL + 1))
            store_tile(Chunk(PL, 0), (N - 2 * P) * 2 * D)

            n = turns(sp)
            sp.wait_ge(pads_in, 96)

            def load_chunk(c, s):
                first = sp.value_load(base_i[0:1, bass.ds(s, 1)], min_val=0, max_val=EP - C - 2)
                second = sp.snap(first + 1)
                node = sp.value_load(nb_i[0:1, bass.ds(s + 1, 1)], min_val=0, max_val=(N - P) * D)
                sp.wait_ge(e1_done, c.done())
                sp.nop(nofuse=True)
                sp.dma_start(dst_l[:, c.par], bass.AP(dst_pad.tensor, first, [[G, P], [1, G + 2]]))\
                    .then_inc(idx_in, 16)
                sp.dma_start(src_l[:, c.par], bass.AP(src_pad.tensor, second, [[G, P], [1, G]]))\
                    .then_inc(idx_in, 16)
                sp.wait_ge(res_done, c.done())
                sp.nop(nofuse=True)
                sp.dma_start(xw[:, c.par], rows1(x, node)).then_inc(xw_in[c.par], 16)

            def store_window(c, s):
                node = sp.value_load(nb_i[0:1, bass.ds(s, 1)], min_val=0, max_val=(N - P) * D)
                sp.wait_ge(fin_done, c.done(credit=1))
                sp.nop(nofuse=True)
                sp.wait_ge(out_done, c.done(per=16, credit=32))
                sp.nop(nofuse=True)
                sp.dma_start(rows1(out, node), outb[:, c.par]).then_inc(out_done, 16)

            load_chunk(Chunk(0, 0), 0)
            load_chunk(Chunk(0, 1), 1)
            with sp.Fori(0, n) as i:
                for b in range(2):
                    c = Chunk(i, b)
                    load_chunk(c.next().next(), 2 * i + b + 2)
                    store_window(c.prev(), 2 * i + b)
            store_window(Chunk(n, -1), 2 * n)
            sp.wait_ge(out_done, n * 32 + 48)
            sp.nop(nofuse=True)

        @block.gpsimd
        def _(pool):
            step = [0]

            def link(ins):
                step[0] += 1
                ins.then_inc(pool_step, 1)
                pool.wait_ge(pool_step, step[0])

            pool.memset(padi[:, 0:TAIL // 16], 1 << 20).then_inc(pad_tile, 1)
            pool.memset(padi[:, TAIL // 16:], 0).then_inc(pad_tile, 1)
            pool.memset(rfold[:, :, :, :], 0.0).then_inc(rz, 1)
            pool.memset(ones[:, :], 1.0).then_inc(consts, 1)
            link(pool.memset(ident[:, :], 0.0))
            pool.affine_select(out=ident[:, :], in_=ident[:, :], compare_op=ALU.not_equal, fill=1.0,
                               base=0, pattern=[[-1, P]], channel_multiplier=1).then_inc(consts, 1)
            pool.iota(thr[:, 0:1], pattern=[[0, 1]], base=0, channel_multiplier=P,
                      allow_small_or_imprecise_dtypes=True).then_inc(consts, 1)
            pool.iota(thr[:, 1:2], pattern=[[0, 1]], base=0, channel_multiplier=1,
                      allow_small_or_imprecise_dtypes=True).then_inc(consts, 1)
            pool.iota(iota_s[:, :], pattern=[[1, SM]], base=0, channel_multiplier=0,
                      allow_small_or_imprecise_dtypes=True).then_inc(consts, 1)
            pool.iota(iota_c[:, :], pattern=[[C, J]], base=C, channel_multiplier=0,
                      allow_small_or_imprecise_dtypes=True).then_inc(consts, 1)
            pool.iota(iota_n[:, :], pattern=[[1, P]], base=0, channel_multiplier=0,
                      allow_small_or_imprecise_dtypes=True).then_inc(consts, 1)
            link(pool.memset(lower[:, :], 1.0))
            pool.affine_select(out=lower[:, :], in_=lower[:, :], compare_op=ALU.is_gt, fill=0.0,
                               base=0, pattern=[[1, P]], channel_multiplier=-1).then_inc(consts, 1)
            link(pool.memset(diff[:, :], 0.0))
            link(pool.affine_select(out=diff[:, :], in_=diff[:, :], compare_op=ALU.not_equal, fill=1.0,
                                    base=-1, pattern=[[-1, P]], channel_multiplier=1))
            pool.affine_select(out=diff[:, :], in_=diff[:, :], compare_op=ALU.not_equal, fill=-1.0,
                               base=0, pattern=[[-1, P]], channel_multiplier=1).then_inc(consts, 1)
            link(pool.memset(lastw[:, :], 0.0))
            pool.affine_select(out=lastw[:, :], in_=lastw[:, :], compare_op=ALU.not_equal, fill=1e6,
                               base=1 - W, pattern=[[0, 1]], channel_multiplier=1).then_inc(consts, 1)
            link(pool.memset(notlast[:, :], 1.0))
            pool.affine_select(out=notlast[:, :], in_=notlast[:, :], compare_op=ALU.not_equal, fill=0.0,
                               base=1 - P, pattern=[[0, 1]], channel_multiplier=1).then_inc(consts, 1)
            link(pool.memset(notfirst[:, :], 0.0))
            pool.affine_select(out=notfirst[:, :], in_=notfirst[:, :], compare_op=ALU.not_equal, fill=-BIG,
                               base=0, pattern=[[0, 1]], channel_multiplier=1).then_inc(consts, 1)
            pool.wait_ge(rows_idx, 1)
            pool.indirect_dma_start(out=drow[:, :], out_offset=None,
                                    in_=dst.rearrange("(a b) -> a b", b=RC),
                                    in_offset=bass.IndirectOffsetOnAxis(ap=rowi[:, 0:1], axis=0),
                                    bounds_check=ROWS - 1, oob_is_err=False).then_inc(drow_in, 16)
            for b in range(2):
                pool.memset(kv[:, b], 0.0).then_inc(setup, 1)
            pool.wait_ge(kv_out[0], 16 * (PL + 2))
            pool.wait_ge(kv_out[1], 16 * (PL + 1))
            pool.wait_ge(setup, 2)
            n = turns(pool)
            last_row = pool.to_reg(N - 1)

            def gather(c):
                pool.wait_ge(e1_done, c.done(credit=1))
                pool.nop(nofuse=True)
                for q, (g0, gn) in enumerate(PAIRS):
                    pool.wait_ge(w_ready, c.done(per=NQ, credit=q + 1, back=NQ))
                    pool.nop(nofuse=True)
                    for g in range(g0, g0 + gn):
                        pool.indirect_dma_start(
                            out=kv[:, c.par, g, :], out_offset=None, in_=kv_dram,
                            in_offset=bass.IndirectOffsetOnAxis(ap=gidx[:, c.par, g:g + 1], axis=0),
                            bounds_check=last_row, oob_is_err=False).then_inc(gat[c.par][q], 16)

            gather(Chunk(0, 0))
            with pool.Fori(0, n) as i:
                for b in range(2):
                    gather(Chunk(i, b).next())

        @block.tensor
        def _(pe):
            pe.wait_ge(wts_in, N_WTS)
            pe.wait_ge(consts, N_CONST)
            pe.wait_ge(fold_in, 1)
            for k in range(4):
                for a in range(2):
                    r = rfold[:, k, a] if k < 3 else ident[:, :]
                    for kh in range(2):
                        nc.tensor.matmul(bank[2 * k][:, kh * D + a * P:kh * D + (a + 1) * P],
                                         wl[:, k, a, kh * P:(kh + 1) * P], r, start=True, stop=True)
                    last = nc.tensor.matmul(bank[2 * k + 1][:, a * P:(a + 1) * P], bwide[:, k, a], r,
                                            start=True, stop=True)
                last.then_inc(fold_mm, 1)
            pe.wait_ge(fold_cp, 4)
            pe.wait_ge(tab_in, 1)
            nc.tensor.matmul(bank[0][:, 0:ROWS], ones[0:1, :], rowf[0:1, 0:ROWS], start=True, stop=True)\
                .then_inc(tab_mm, 1)
            pe.wait_ge(tab_in, 2)
            nc.tensor.matmul(bank[1][:, 0:1], diff[:, :], tcol[:, 2:3], start=True, stop=True).then_inc(tab_mm, 1)
            pe.wait_ge(tab_in, 3)
            nc.tensor.matmul(bank[2][:, 0:1], lower[0:W, :], tcol[0:W, 4:5], start=True, stop=True)
            nc.tensor.matmul(bank[2][:, 1:2], ones[0:W, :], tcol[0:W, 4:5], start=True, stop=True)\
                .then_inc(tab_mm, 1)
            pe.wait_ge(tab_in, 4)
            nc.tensor.matmul(bank[3][:, 0:SM], cmp[0:W, 0:P], act_a[0:W, :], start=True, stop=True)
            nc.tensor.matmul(bank[4][:, 0:SM], cmp[0:W, P:2 * P], act_a[0:W, :], start=True, stop=True)\
                .then_inc(tab_mm, 1)

            def project(t):
                pe.wait_ge(x_in[t.par], t.landed())
                pe.wait_ge(x_Tc, t.done())
                for j in range(2):
                    for kh in range(2):
                        last = nc.tensor.transpose(bank[0][:, (2 * j + kh) * P:(2 * j + kh + 1) * P],
                                                   xt[:, t.par, j, kh * P:(kh + 1) * P], ident[:, :])
                last.then_inc(x_T, 1)
                pe.wait_ge(x_Tc, t.done(credit=1))
                pe.wait_ge(kv_add, t.done())
                for j in range(2):
                    for kh in range(2):
                        last = nc.tensor.matmul(bank[2 + 2 * t.par + j][:, :],
                                                xT[:, t.par, (2 * j + kh) * P:(2 * j + kh + 1) * P],
                                                wkv[:, kh], start=(kh == 0), stop=(kh == 1))
                last.then_inc(kv_mm, 1)

            pe.wait_ge(tables, 1)
            with pe.Fori(0, PL) as i:
                for b in range(2):
                    project(Chunk(i, b))
            project(Chunk(PL, 0))
            pe.wait_ge(kv_add, 2 * PL + 3)

            def window_q(c):
                pe.wait_ge(xw_in[c.par], c.landed())
                pe.wait_ge(q_done, c.done(credit=1))
                for kh in range(2):
                    last = nc.tensor.transpose(ps_win[:, kh * P:(kh + 1) * P], xw[:, c.par, kh * P:(kh + 1) * P],
                                               ident[:, :])
                last.then_inc(win_T, 1)
                pe.wait_ge(win_Tc, c.done())
                for kh in range(2):
                    last = nc.tensor.matmul(ps_win[:, D:2 * D], xwT[:, kh * P:(kh + 1) * P], wq[:, kh],
                                            start=(kh == 0), stop=(kh == 1))
                last.then_inc(win_q, 1)

            def spread_q(c, q):
                if q == 0:
                    pe.wait_ge(q_done, c.done(credit=2))
                pe.wait_ge(q_used, c.done(per=NQ, credit=q + 1, back=NQ))
                g0, gn = PAIRS[q]
                if g0 % 4 == 0:
                    pe.wait_ge(oh_Tc, c.done(per=NT, credit=2 + g0 // 4 + 1, back=NT))
                for g in range(g0, g0 + gn):
                    last = nc.tensor.matmul(ps_q[(c.par + q) % 2][:, (g - g0) * D:(g - g0 + 1) * D],
                                            onehotT[:, c.par, g], qf[:, c.par], start=True, stop=True)
                last.then_inc(q_edge, 1)

            def transpose_onehots(c, t):
                g0, gn = TGROUPS[t]
                if t == 0:
                    pe.wait_ge(oh_ready, c.done())
                if t == NT - 1:
                    pe.wait_ge(masks_ready, c.done())
                pe.wait_ge(oh_Tc, c.done(per=NT, credit=t + 1, back=NT))
                for g in range(g0, g0 + gn):
                    last = nc.tensor.transpose(ps_t[(c.par + t) % 2][:, (g - g0) * P:(g - g0 + 1) * P],
                                               onehot[:, c.par, g], ident[:, :])
                if t == NT - 1:
                    for m in range(2):
                        last = nc.tensor.transpose(ps_t[(c.par + t) % 2][0:H, (m + 2) * P:(m + 3) * P],
                                                   mlc[:, m], ident[:, :])
                last.then_inc(oh_T, 1)

            def finish_T(c):
                pe.wait_ge(tn_ready, c.done(credit=1))
                for kh in range(2):
                    last = nc.tensor.transpose(ps_fin[:, kh * P:(kh + 1) * P], tn[:, kh * P:(kh + 1) * P],
                                               ident[:, :])
                last.then_inc(tn_T, 1)

            def finish_mm(c):
                pe.wait_ge(tn_Tc, c.done(credit=1))
                for kh in range(2):
                    last = nc.tensor.matmul(ps_fin[:, D:2 * D], tT[:, kh * P:(kh + 1) * P], wa[:, kh],
                                            start=(kh == 0), stop=(kh == 1))
                last.then_inc(y_mm, 1)

            def aggregate(c, q):
                pe.wait_ge(w_ready, c.done(per=NQ, credit=NQ + q + 1))
                g0, gn = PAIRS[q]
                for g in range(g0, g0 + gn):
                    last = nc.tensor.matmul(ps_agg[:, 0:WX], onehot[:, c.par, g], wv[:, g],
                                            start=(g == 0), stop=(g == G - 1))
                if q == NQ - 1:
                    last.then_inc(agg_done, 1)

            c0 = Chunk(0, 0)
            window_q(c0)
            for t in range(NT):
                transpose_onehots(c0, t)
            for q in range(NQ):
                spread_q(c0, q)
            n = turns(pe)
            with pe.Fori(0, n) as i:
                for b in range(2):
                    c = Chunk(i, b)
                    pe.wait_ge(tail_ready, c.done())
                    nc.tensor.transpose(TAILT, bmax[:, :, G - 1], ident[:, :])
                    nc.tensor.transpose(HEADT, bmax[:, :, 0], ident[:, :]).then_inc(tail_T, 1)
                    window_q(c.next())
                    transpose_onehots(c.next(), 0)
                    pe.wait_ge(ut_ready, c.done())
                    nc.tensor.transpose(CARRYT[0], ut[:, 0], ident[:, :])
                    nc.tensor.transpose(CARRYT[1], ut[:, 1], ident[:, :]).then_inc(carry_T, 1)
                    transpose_onehots(c.next(), 1)
                    finish_T(c.prev())
                    pe.wait_ge(agg_read, c.done())
                    for q in range(NQ):
                        spread_q(c.next(), q)
                        aggregate(c, q)
                        if q == 0:
                            finish_mm(c.prev())
                        if q + 2 < NT:
                            transpose_onehots(c.next(), q + 2)
            finish_T(Chunk(n, -1))
            finish_mm(Chunk(n, -1))

        @block.scalar
        def _(act):
            act.wait_ge(wts_in, N_WTS)
            nc.scalar.activation(skc[:, 1:2], skc[:, 0:1], ACT.Exp, scale=-1.0).then_inc(skip_exp, 1)

            def copy_xT(t):
                act.wait_ge(x_T, t.done(credit=2))
                act.wait_ge(kv_mm, t.done())
                nc.scalar.activation(xT[:, t.par], bank[0][:, :], ACT.Copy).then_inc(x_Tc, 1)

            with act.Fori(0, PL) as i:
                for b in range(2):
                    copy_xT(Chunk(i, b))
            copy_xT(Chunk(PL, 0))

            def copy_xwT(c):
                act.wait_ge(win_T, c.done())
                nc.scalar.activation(xwT[:, :], ps_win[:, 0:D], ACT.Copy).then_inc(win_Tc, 1)

            def copy_onehotT(c, t):
                g0, gn = TGROUPS[t]
                act.wait_ge(oh_T, c.done(per=NT, credit=t + 1, back=NT))
                src_bank = ps_t[(c.par + t) % 2]
                if t == NT - 1:
                    nc.scalar.activation(mlT[:, c.par, 0], src_bank[0:H, 2 * P:3 * P], ACT.Copy)
                    nc.scalar.activation(linkT[:, c.par, 0:P], src_bank[0:H, 3 * P:4 * P], ACT.Copy).then_inc(mask_T, 1)
                nc.scalar.activation(onehotT[:, c.par, g0:g0 + gn].rearrange("p g k -> p (g k)"),
                                     src_bank[:, 0:gn * P], ACT.Copy).then_inc(oh_Tc, 1)

            def copy_tT(c):
                act.wait_ge(tn_T, c.done(credit=1))
                nc.scalar.activation(tT[:, :], ps_fin[:, 0:D], ACT.Copy).then_inc(tn_Tc, 1)

            def statistics(c):
                act.wait_ge(yy_ready, c.done(credit=1))
                nc.scalar.activation(scratch[:, :], yy[:, :], ACT.Copy, accum_out=ln[:, 0:1]).then_inc(ln_step, 1)
                act.wait_ge(ln_step, c.done(per=4, credit=1))
                nc.scalar.activation(ln[:, 1:2], ln[:, 0:1], ACT.Copy, scale=-1.0 / D).then_inc(ln_step, 1)
                act.wait_ge(ln_step, c.done(per=4, credit=2))
                nc.scalar.activation(scratch[:, :], yy[:, :], ACT.Square, bias=ln[:, 1:2],
                                     accum_out=ln[:, 2:3]).then_inc(ln_step, 1)
                act.wait_ge(ln_step, c.done(per=4, credit=3))
                nc.scalar.activation(ln[:, 3:4], ln[:, 2:3], ACT.Ln, bias=eps_c[:, :], scale=1.0 / D)\
                    .then_inc(ln_step, 1)
                act.wait_ge(ln_step, c.done(per=4, credit=4))
                nc.scalar.activation(ln[:, 4:5], ln[:, 3:4], ACT.Exp, scale=-0.5).then_inc(rs_ready, 1)

            copy_xwT(Chunk(0, 0))
            for t in range(NT):
                copy_onehotT(Chunk(0, 0), t)
            n = turns(act)

            def merge_factors(c):
                act.wait_ge(dab_ready, c.done(credit=1))
                nc.scalar.activation(ab[:, :, :], dab[:, :, :], ACT.Exp).then_inc(ab_ready, 1)

            with act.Fori(0, n) as i:
                for b in range(2):
                    c = Chunk(i, b)
                    merge_factors(c.prev())
                    copy_xwT(c.next())
                    copy_onehotT(c.next(), 0)
                    copy_onehotT(c.next(), 1)
                    copy_tT(c.prev())
                    act.wait_ge(d_ready, c.done())
                    nc.scalar.activation(heads(wv[:, :, 0:WC])[:, :, :, DK], dexp[:, :, :], ACT.Exp)\
                        .then_inc(ex_ready, 1)
                    for t in range(2, NT):
                        copy_onehotT(c.next(), t)
                    statistics(c.prev())
            merge_factors(Chunk(n, -1))
            copy_tT(Chunk(n, -1))
            statistics(Chunk(n, -1))

        @block.vector
        def _(v):
            step = [0]

            def link(ins):
                step[0] += 1
                ins.then_inc(dve_setup, 1)
                v.wait_ge(dve_setup, step[0])

            v.wait_ge(consts, N_CONST)
            v.wait_ge(wts_in, N_WTS)
            v.wait_ge(rz, 1)
            for k in range(4):
                for a in range(2):
                    link(v.tensor_copy(bwide[:, k, a], bcol[:, k, a:a + 1].to_broadcast([P, P])))
            for a in range(2):
                link(v.tensor_scalar(rfold[:, 2, a], ident[:, :], pcol[:, a:a + 1], 1.0 / math.sqrt(DK),
                                     ALU.mult, ALU.mult))
            link(v.memset(ys[:, :], -BIG))
            v.memset(xs[:, :], -BIG).then_inc(fold_in, 1)
            v.wait_ge(skip_exp, 1)
            link(v.tensor_scalar(skc[:, 2:3], skc[:, 1:2], 1.0, None, ALU.add))
            link(v.reciprocal(skc[:, 3:4], skc[:, 2:3]))
            link(v.tensor_scalar(skc[:, 4:5], skc[:, 3:4], -1.0, 2.0, ALU.mult, ALU.add))
            for k, (wt, off, bt) in enumerate(((wkv, 0, bkv), (wkv, D, bkv), (wq, 0, bqb), (wa, 0, bab))):
                v.wait_ge(fold_mm, k + 1)
                link(v.tensor_copy(wt[:, :, off:off + D], bank[2 * k][:, :].rearrange("p (a c) -> p a c", a=2)))
                if k < 3:
                    last = v.tensor_copy(bt[:, off:off + D], bank[2 * k + 1][:, 0:D])
                else:
                    last = v.tensor_scalar(bt[:, :], bank[2 * k + 1][:, 0:D], skc[:, 3:4], None, ALU.mult)
                last.then_inc(fold_cp, 1)
            v.wait_ge(row_in, 16)
            link(v.memset(rowf[:, :], 0.0))
            link(v.tensor_copy(rowf[0:1, 0:ROWS], row1[0:1, 0:ROWS]))
            link(v.tensor_scalar(tcol[:, 0:1], thr[:, 1:2], float(W), 1e6, ALU.is_ge, ALU.mult))
            link(v.tensor_scalar(tcol[:, 1:2], thr[:, 0:1], float(N - P), None, ALU.min))
            link(v.tensor_tensor(tcol[:, 0:1], tcol[:, 0:1], tcol[:, 1:2], ALU.add))
            v.memset(outb[:, :, :], 0.0).then_inc(tab_in, 1)
            v.wait_ge(tab_mm, 1)
            link(v.tensor_scalar(cmp[:, 0:ROWS], bank[0][:, 0:ROWS], tcol[:, 0:1], None, ALU.is_lt))
            link(v.tensor_reduce(tcol[:, 8:9], cmp[:, 0:ROWS], AX.X, ALU.add))
            link(v.tensor_scalar(tcol[:, 9:10], tcol[:, 8:9], -1.0, 0.0, ALU.add, ALU.max))
            v.tensor_copy(rowi[:, :], tcol[:, 9:10]).then_inc(rows_idx, 1)
            v.wait_ge(drow_in, 16)
            link(v.tensor_scalar(cmp[:, 0:RC], drow[:, :], tcol[:, 0:1], None, ALU.is_lt))
            link(v.tensor_reduce(tcol[:, 10:11], cmp[:, 0:RC], AX.X, ALU.add))
            v.scalar_tensor_tensor(out=tcol[:, 2:3], in0=tcol[:, 9:10], scalar=float(RC), in1=tcol[:, 10:11],
                                   op0=ALU.mult, op1=ALU.add).then_inc(tab_in, 1)
            v.wait_ge(tab_mm, 2)
            v.wait_ge(tab_in, 2)
            link(v.tensor_copy(tcol[:, 3:4], bank[1][:, 0:1]))
            link(v.tensor_scalar(cmp[:, 0:J], iota_c[:, :], tcol[:, 3:4], None, ALU.is_lt))
            link(v.tensor_reduce(tcol[:, 11:12], cmp[:, 0:J], AX.X, ALU.add))
            v.tensor_scalar(tcol[:, 4:5], tcol[:, 11:12], 1.0, None, ALU.add).then_inc(tab_in, 1)
            v.wait_ge(tab_mm, 3)
            v.wait_ge(tab_in, 3)
            link(v.tensor_copy(tcol[:, 5:6], bank[2][:, 0:1]))
            link(v.tensor_tensor(tcol[:, 12:13], tcol[:, 5:6], tcol[:, 4:5], ALU.add))
            link(v.tensor_tensor(tcol[:, 6:7], tcol[:, 12:13], lastw[:, :], ALU.add))
            link(v.tensor_scalar(act_b[:, :], iota_s[:, :], tcol[:, 6:7], None, ALU.is_ge))
            link(v.scalar_tensor_tensor(out=act_a[:, :], in0=iota_s[:, :], scalar=tcol[:, 5:6], in1=act_b[:, :],
                                        op0=ALU.is_ge, op1=ALU.subtract))
            link(v.scalar_tensor_tensor(out=tcol[:, 7:8], in0=tcol[:, 5:6], scalar=-float(C), in1=tcol[:, 2:3],
                                        op0=ALU.mult, op1=ALU.add))
            link(v.tensor_scalar(cmp[:, 0:P], ones[:, :], tcol[:, 0:1], None, ALU.mult))
            link(v.tensor_scalar(cmp[:, P:2 * P], ones[:, :], tcol[:, 7:8], None, ALU.mult))
            link(v.tensor_copy(tcol[:, 13:14], bank[2][:, 1:2]))
            link(v.tensor_scalar(act_b[:, 0:SM // 2], iota_s[:, 0:SM // 2], 2.0, tcol[:, 13:14], ALU.mult,
                                 ALU.is_lt))
            link(v.tensor_reduce(tcol[:, 14:15], act_b[:, 0:SM // 2], AX.X, ALU.add))
            link(v.tensor_copy(cnt_i[0:1, 0:1], tcol[0:1, 14:15]))
            v.memset(yy[:, :], 0.0).then_inc(tab_in, 1)
            v.wait_ge(tab_mm, 4)
            link(v.tensor_copy(nb_t[:, :], bank[3][:, 0:SM]))
            link(v.scalar_tensor_tensor(out=base_t[:, :], in0=iota_s[:, :], scalar=float(C), in1=bank[4][:, 0:SM],
                                        op0=ALU.mult, op1=ALU.add))
            link(v.tensor_copy(base_i[0:1, :], base_t[0:1, :]))
            link(v.memset(nb_i[0:1, 0:1], 0))
            link(v.tensor_scalar(nb_i[0:1, 1:SM + 1], nb_t[0:1, :], float(D), None, ALU.mult))
            link(v.memset(nw_t[:, :], -BIG))
            link(v.tensor_tensor(nw_t[:, 1:SM], nb_t[:, 1:SM], nb_t[:, 0:SM - 1], ALU.is_equal))
            link(v.tensor_scalar(nw_t[:, 1:SM], nw_t[:, 1:SM], BIG, -BIG, ALU.mult, ALU.add))
            link(v.memset(runs[:, :, :], -BIG))
            link(v.memset(linkT[:, :, :], -BIG))
            link(v.memset(ut[:, :, :], 0.0))
            link(v.memset(nwc[:, :], 0.0))
            link(v.memset(eps_c[:, :], EPS))
            link(v.memset(mrun[:, :], -BIG))
            link(v.memset(state[:, :, :], 0.0))
            link(v.memset(ab[:, :, :], 0.0))
            link(v.memset(res[:, :, :], 0.0))
            link(v.memset(ps_agg[:, :], 0.0))
            for k, (s, by) in enumerate(((x_T, 2), (x_Tc, 1), (kv_mm, 2), (kv_out[0], 16), (kv_out[1], 16),
                          (kv_add, 2), (e1_done, 1), (q_done, 2), (res_done, 2), (out_done, 32), (w_ready, 2 * NQ), (q_used, 2),
                          (oh_Tc, 2), (agg_done, 1))):
                v.memset(cell[:, k:k + 1], 0.0).then_inc(s, by)
            v.memset(cell[:, 15:16], 0.0).then_inc(tables, 1)

            def add_bias(t):
                v.wait_ge(kv_mm, t.done(credit=2))
                v.wait_ge(kv_out[t.par], t.landed())
                for j in range(2):
                    last = v.tensor_tensor(kvs[:, t.par, j], bank[2 + 2 * t.par + j][:, :], bkv[:, :], ALU.add)
                last.then_inc(kv_add, 1)

            with v.Fori(0, PL) as i:
                for b in range(2):
                    add_bias(Chunk(i, b))
            add_bias(Chunk(PL, 0))

            def lapped(ins):
                count[0] += 1
                ins.then_inc(dstep, 1)
                return count[0]

            def settle(c, k):
                v.wait_ge(dstep, c.done(per=K_DVE, credit=STEPS0 + k, back=K_DVE))

            def dlink(c, ins):
                settle(c, lapped(ins))

            def edges_in(c, at):
                p = c.par
                v.wait_ge(idx_in, c.done(per=32))
                dlink(at, v.tensor_copy(nbc[:, :], nb_t[:, bass.ds(c.number(), 1)]))
                dlink(at, v.tensor_scalar(rel[:, p], dst_l[:, p], nbc[:, :], None, ALU.subtract))
                dlink(at, v.tensor_scalar(off_w[:, :], rel[:, p, 1:G + 1], float(P), FAR, ALU.is_ge, ALU.mult))
                v.tensor_tensor(gidx[:, p], off_w[:, :], src_l[:, p], ALU.add).then_inc(e1_done, 1)

            def one_hots(c):
                v.tensor_tensor(onehot[:, c.par], bc(iota_n[:, :], 1, G), bc(rel[:, c.par, 1:G + 1], 2, P),
                                ALU.is_equal).then_inc(oh_ready, 1)

            def masks(c, at):
                p = c.par
                lapped(v.tensor_copy(nwc[:, p:p + 1], nw_t[:, bass.ds(c.number(), 1)]))
                lapped(v.tensor_scalar(headm[:, p, 0], rel[:, p, 1:G + 1], rel[:, p, 1:2], BIG, ALU.is_equal, ALU.mult))
                lapped(v.tensor_scalar(headm[:, p, 1], rel[:, p, 1:G + 1], rel[:, p, G:G + 1], BIG,
                                       ALU.is_equal, ALU.mult))
                dlink(at, v.tensor_tensor(same[:, :], rel[:, p, 1:G + 2], rel[:, p, 0:G + 1], ALU.is_equal))
                lapped(v.tensor_scalar(headm[:, p], headm[:, p], -BIG, None, ALU.add))
                dlink(at, v.tensor_tensor(same[:, G:G + 1], same[:, G:G + 1], notlast[:, :], ALU.mult))
                dlink(at, v.tensor_scalar(msk[:, :], same[:, :], BIG, -BIG, ALU.mult, ALU.add))
                lapped(v.tensor_scalar(lastedge[:, p], same[:, 1:G + 1], -1.0, 1.0, ALU.mult, ALU.add))
                lapped(v.tensor_copy(runs[:, p, 0:H * G].rearrange("p (h g) -> p h g", h=H)[:, :, 1:G],
                                     bc(msk[:, 1:G], 1, H)))
                lapped(v.tensor_reduce(mlc[:, 0], bc(msk[:, 1:G], 1, H), AX.X, ALU.min))
                v.tensor_tensor(mlc[:, 1], msk[:, 0:1].to_broadcast([P, H]), notfirst[:, :].to_broadcast([P, H]),
                                ALU.min).then_inc(masks_ready, 1)

            def window_q_in(c):
                v.wait_ge(win_q, c.done())
                v.tensor_tensor(qf[:, c.par], ps_win[:, D:2 * D], bqb[:, :], ALU.add).then_inc(q_done, 1)

            def residual(c):
                v.wait_ge(xw_in[c.par], c.landed())
                v.scalar_tensor_tensor(out=res[:, c.par], in0=xw[:, c.par], scalar=skc[:, 4:5], in1=bab[:, :],
                                       op0=ALU.mult, op1=ALU.add).then_inc(res_done, 1)

            def multiply(c, q):
                g0, gn = PAIRS[q]
                v.wait_ge(gat[c.par][q], c.landed(per=16 * gn))
                v.wait_ge(q_edge, c.done(per=NQ, credit=q + 1, back=NQ))
                v.tensor_tensor(prod[:, q % 3, 0:gn], kv[:, c.par, g0:g0 + gn, 0:D],
                                ps_q[(c.par + q) % 2][:, 0:gn * D].rearrange("p (g d) -> p g d", d=D),
                                ALU.mult).then_inc(q_used, 1)

            def scores(c, q):
                g0, gn = PAIRS[q]
                v.wait_ge(q_used, c.done(per=NQ, credit=2 + q + 1, back=NQ))
                return lapped(v.tensor_reduce(score[:, :, g0:g0 + gn].rearrange("p h g -> p g h"),
                                              prod[:, q % 3, 0:gn].rearrange("p g (h d) -> p g h d", d=DK),
                                              AX.X, ALU.add))

            def merge_maxima(c, at):
                v.wait_ge(agg_done, c.done(credit=1))
                dlink(at, v.tensor_scalar(pres[:, :], NMAX[:, H:H + 1], BIG, -BIG, ALU.mult, ALU.add))
                lapped(v.tensor_scalar(m4[:, 1], mrun[:, :], nwc[:, c.par:c.par + 1], None, ALU.add))
                dlink(at, v.tensor_scalar(m4[:, 0], NMAX[:, 0:H], pres[:, :], None, ALU.add))
                dlink(at, v.tensor_tensor(mrun[:, :], m4[:, 0], m4[:, 1], ALU.max))
                v.tensor_tensor(dab[:, 0], m4[:, 1], mrun[:, :], ALU.subtract)
                v.tensor_tensor(dab[:, 1], m4[:, 0], mrun[:, :], ALU.subtract).then_inc(dab_ready, 1)

            def merge(c, at):
                v.wait_ge(ab_ready, c.done(credit=1))
                v.tensor_tensor(part[:, :, :], heads(ps_agg[:, 0:WC]), bc(ab[:, 1], 2, DK + 1), ALU.mult)
                v.tensor_tensor(state[:, :, :], state[:, :, :], bc(ab[:, 0], 2, DK + 1), ALU.mult).then_inc(agg_read, 1)
                v.wait_ge(agg_read, c.done(credit=1))
                dlink(at, v.tensor_tensor(state[:, :, :], state[:, :, :], part[:, :, :], ALU.add))
                dlink(at, v.scalar_tensor_tensor(out=zz[:, 0], in0=state[:, :, DK], scalar=0.0, in1=state[:, :, DK],
                                                 op0=ALU.is_equal, op1=ALU.add))
                dlink(at, v.reciprocal(zz[:, 1], zz[:, 0]))
                v.tensor_tensor(tn[:, :].rearrange("p (h d) -> p h d", h=H), state[:, :, 0:DK],
                                bc(zz[:, 1], 2, DK), ALU.mult).then_inc(tn_ready, 1)

            def weigh(c, q):
                g0, gn = PAIRS[q]
                if q == 0:
                    v.wait_ge(ex_ready, c.done())
                w4 = heads(wv[:, g0:g0 + gn, 0:WC])
                v.tensor_tensor(w4[:, :, :, 0:DK],
                                kv[:, c.par, g0:g0 + gn, D:2 * D].rearrange("p g (h d) -> p g h d", d=DK),
                                bc(w4[:, :, :, DK], 3, DK), ALU.mult).then_inc(w_ready, 1)

            def finish(c, at):
                v.wait_ge(y_mm, c.done(credit=1))
                v.wait_ge(out_done, c.done(per=16, credit=16))
                v.scalar_tensor_tensor(out=yy[:, :], in0=ps_fin[:, D:2 * D], scalar=skc[:, 3:4],
                                       in1=res[:, c.par], op0=ALU.mult, op1=ALU.add).then_inc(yy_ready, 1)

            def normalise(c, at):
                v.wait_ge(rs_ready, c.done(credit=1))
                lapped(v.tensor_scalar(ln[:, 5:6], ln[:, 2:3], 1.0 / D, EPS, ALU.mult, ALU.add))
                dlink(at, v.tensor_tensor(ln[:, 6:7], ln[:, 4:5], ln[:, 4:5], ALU.mult))
                dlink(at, v.scalar_tensor_tensor(out=ln[:, 7:8], in0=ln[:, 6:7], scalar=-0.5, in1=ln[:, 5:6],
                                                 op0=ALU.mult, op1=ALU.mult))
                dlink(at, v.scalar_tensor_tensor(out=ln[:, 8:9], in0=ln[:, 7:8], scalar=1.5, in1=ln[:, 4:5],
                                                 op0=ALU.add, op1=ALU.mult))
                v.tensor_scalar(outb[:, c.par], yy[:, :], ln[:, 1:2], ln[:, 8:9], ALU.add, ALU.mult)\
                    .then_inc(fin_done, 1)

            def flat(t):
                return t.rearrange("p h g -> p (h g)")

            def back(t, width, first, n, rows=None):
                return bass.AP(t, first, [[width, rows or t.shape[0]], [-1, n]])

            def maxima(c, at):
                b = c.par
                dlink(at, v.tensor_tensor_scan(flat(fmax[:, :, :]), runs[:, b, 0:H * G], flat(score[:, :, :]), -BIG,
                                               ALU.add, ALU.max))
                v.tensor_tensor_scan(back(bmax, H * G, H * G - 1, H * G),
                                     back(runs, 2 * (H * G + 1), b * (H * G + 1) + H * G, H * G),
                                     back(fmax, H * G, H * G - 1, H * G), -BIG, ALU.add, ALU.max)\
                    .then_inc(tail_ready, 1)
                v.wait_ge(mask_T, c.done())
                lapped(v.tensor_tensor(passT[:, 0], mlT[:, b, 0], linkT[:, b, 0:P], ALU.add))
                dlink(at, v.tensor_tensor(passT[:, 1], mlT[:, b, 0], linkT[:, b, 1:P + 1], ALU.add))
                merge_maxima(c.prev(), at)
                one_hots(c.next())
                v.wait_ge(tail_T, c.done())
                lapped(v.tensor_tensor_scan(xs[:, 1:P + 1], passT[:, 0], TAILT, -BIG, ALU.add, ALU.max))
                dlink(at, v.tensor_tensor_scan(back(ys, P + 1, P - 1, P), back(passT, 2 * P, 2 * P - 1, P),
                                               back(ps_small, 512, 2 * P - 1, P, H), -BIG, ALU.add, ALU.max))
                v.tensor_tensor(ut[0:H, 0], xs[:, 0:P], linkT[:, b, 0:P], ALU.add)
                v.tensor_tensor(ut[0:H, 1], ys[:, 1:P + 1], linkT[:, b, 1:P + 1], ALU.add).then_inc(ut_ready, 1)
                merge(c.prev(), at)
                masks(c.next(), at)
                v.wait_ge(carry_T, c.done())
                v.wait_ge(tail_ready, c.done())
                for k in range(2):
                    last = lapped(v.tensor_tensor(tu[:, k], bc(CARRYT[k][:, 0:H], 2, G), bc(headm[:, b, k], 1, H),
                                                  ALU.add))
                settle(at, last)
                dlink(at, v.tensor_tensor(tu[:, 0], tu[:, 0], tu[:, 1], ALU.max))
                dlink(at, v.tensor_tensor(tu[:, 0], tu[:, 0], bmax[:, :, :], ALU.max))
                v.tensor_tensor(dexp[:, :, :], score[:, :, :].rearrange("p h g -> p g h"),
                                tu[:, 0].rearrange("p h g -> p g h"), ALU.subtract).then_inc(d_ready, 1)
                v.tensor_tensor(wv[:, :, WC:WC + H], tu[:, 0].rearrange("p h g -> p g h"), bc(lastedge[:, b], 2, H),
                                ALU.mult)
                v.tensor_copy(wv[:, :, WX - 1], lastedge[:, b])
                edges_in(c.next().next(), at)
                window_q_in(c.next())

            count = [0]
            K_DVE, STEPS0 = 0, 0
            c0 = Chunk(0, 0)
            edges_in(c0, c0)
            edges_in(c0.next(), c0)
            one_hots(c0)
            masks(c0, c0)
            window_q_in(c0)
            residual(c0)

            def score_groups(c, at, between):
                reduced = []
                for q in range(NQ):
                    between(q)
                    if q >= 3:
                        settle(at, reduced[q - 3])
                    multiply(c, q)
                    if q >= 1:
                        reduced.append(scores(c, q - 1))
                settle(at, scores(c, NQ - 1))

            score_groups(c0, c0, lambda q: None)
            K_DVE, STEPS0 = 42, count[0]
            n = turns(v)
            with v.Fori(0, n) as i:
                for b in range(2):
                    c = Chunk(i, b)
                    count[0] = 0
                    maxima(c, c)

                    def between(q):
                        weigh(c, q)
                        if q == 2:
                            finish(c.prev(), c)
                        if q == 4:
                            v.wait_ge(yy_ready, c.done())
                            residual(c.next())
                        if q == 6:
                            normalise(c.prev(), c)

                    score_groups(c.next(), c, between)
                    assert count[0] == K_DVE, count
            end = Chunk(n, -1)
            at = Chunk(n, 0)
            count[0] = 0
            merge_maxima(end, at)
            merge(end, at)
            finish(end, at)
            normalise(end, at)


NAMES = ["x", "src", "dst", "L0_gnn_Wk", "L0_gnn_bk", "L0_gnn_Wq", "L0_gnn_bq", "L0_gnn_Wv", "L0_gnn_bv",
         "L0_gnn_Wa", "L0_gnn_ba", "L0_gnn_rel_att", "L0_gnn_rel_msg", "L0_gnn_rel_pri", "L0_gnn_skip"]


def kernel(**inputs):
    import numpy as np
    import concourse.bacc as bacc
    from concourse.bass_utils import run_bass_kernel_spmd

    nc = bacc.Bacc("TRN2", target_bir_lowering=False, num_devices=1)
    arrays, args = {}, []
    for name in NAMES:
        a = np.ascontiguousarray(inputs[name])
        a = a.reshape(1) if a.ndim == 0 else a
        arrays[name] = a
        args.append(nc.dram_tensor(name, a.shape, mybir.dt.from_np(a.dtype), kind="ExternalInput").ap())
    out = nc.dram_tensor("result", arrays["x"].shape, F32, kind="ExternalOutput").ap()
    gnn_program(nc, *args, out)
    return run_bass_kernel_spmd(nc, [arrays], core_ids=[0]).results[0]["result"]
```

```python
from contextlib import ExitStack
import math

import concourse.bass as bass
from concourse import mybir

ALU = mybir.AluOpType
ACT = mybir.ActivationFunctionType
AX = mybir.AxisListType
F32 = mybir.dt.float32
I32 = mybir.dt.int32

P = 128
G = 17
C = P * G
BIG = 1e30
FAR = float(1 << 22)
EPS = 1e-5
PAIRS = [(g, min(2, G - g)) for g in range(0, G, 2)]
NQ = len(PAIRS)
FOURS = [(g, min(4, G - g)) for g in range(0, G, 4)]
NT = len(FOURS)


class Chunk:

    def __init__(self, turn, off):
        self.turn, self.off, self.par = turn, off, off % 2

    def done(self, per=1, credit=0, back=0):
        return self.turn * (2 * per) + ((self.off + 1) * per + credit - back)

    def landed(self, per=16):
        return self.turn * per + (self.off // 2 + 1) * per

    def number(self):
        return self.turn * 2 + self.off

    def next(self):
        return Chunk(self.turn, self.off + 1)

    def prev(self):
        return Chunk(self.turn, self.off - 1)


def gnn_program(nc, x, src, dst, Wk, bk, Wq, bq, Wv, bv, Wa, ba, rel_att, rel_msg, rel_pri, skip, out):
    N, D = x.shape
    E = src.shape[0]
    H, DK, _ = rel_att.shape
    HPB = P // DK
    assert D == 2 * P and H * DK == D and H == 8
    W = -(-N // P)
    ROWS = 125
    RC = E // ROWS
    assert ROWS * RC == E and W + 1 <= P
    J = E // C + 1
    SM = 2 * ((W + J + 6) // 2)
    WC = H * (DK + 1)
    WX = WC + H + 1
    assert SM <= 512
    TAIL = 16 * (-(-(4 * C + 16) // 16))
    EP = 1 + E + TAIL
    NPAIR = -(-N // (2 * P))
    PL = NPAIR // 2
    assert NPAIR == 2 * PL + 1

    with ExitStack() as ctx:
        def sb(name, shape, dt=F32):
            return ctx.enter_context(nc.sbuf_tensor(name, shape, dt))

        def sem(name):
            return ctx.enter_context(nc.semaphore(name))

        kv_dram = nc.dram_tensor("kv_rows", (N, 2 * D), F32, kind="Internal").ap()
        src_pad = nc.dram_tensor("src_pad", (EP,), I32, kind="Internal").ap()
        dst_pad = nc.dram_tensor("dst_pad", (EP,), I32, kind="Internal").ap()

        bank = [ctx.enter_context(nc.psum_tensor(f"bank{i}", [P, 512], F32)) for i in range(8)]
        ps_t = bank[0:2]
        ps_q = bank[2:4]
        ps_agg = bank[4]
        ps_small = bank[5]
        ps_fin = bank[6]
        ps_win = bank[7]
        TAILT = ps_small[0:H, 0:P]
        HEADT = ps_small[0:H, P:2 * P]
        CARRYT = [ps_small[:, (k + 2) * P:(k + 3) * P] for k in range(2)]
        NMAX = ps_agg[:, WC:WX]

        ident = sb("ident", [P, P])
        wv = sb("wv", [P, G, WX])
        wl = bass.AP(wv, 0, [[G * WX, P], [2 * D, 4], [D, 2], [1, D]])
        rfold = sb("rfold", [P, 3, 2, P])
        bcol = sb("bcol", [P, 4, 2])
        bwide = sb("bwide", [P, 4, 2, P])
        pcol = sb("pcol", [P, 2])
        wkv = sb("wkv", [P, 2, 2 * D])
        bkv = sb("bkv", [P, 2 * D])
        wq = sb("wq", [P, 2, D])
        bqb = sb("bqb", [P, D])
        wa = sb("wa", [P, 2, D])
        bab = sb("bab", [P, D])
        skc = sb("skc", [P, 5])
        iota_n = sb("iota_n", [P, P])
        ends = sb("ends", [P, 2])
        padi = sb("padi", [16, 2 * (TAIL // 16)], I32)

        thr = sb("thr", [P, 4])
        row1 = sb("row1", [1, P], I32)
        rowf = sb("rowf", [1, P])
        ones = sb("ones", [P, P])
        tcol = sb("tcol", [P, 16])
        rowi = sb("rowi", [P, 1], I32)
        lower = sb("lower", [P, P])
        diff = sb("diff", [P, P])
        iota_s = sb("iota_s", [P, SM])
        iota_c = sb("iota_c", [P, J])
        lastw = sb("lastw", [P, 1])
        act_a = sb("act_a", [P, SM])
        act_b = sb("act_b", [P, SM])
        nb_t = sb("nb_t", [P, SM])
        base_t = sb("base_t", [P, SM])
        nw_t = sb("nw_t", [P, SM])
        base_i = sb("base_i", [1, SM], I32)
        nb_i = sb("nb_i", [1, SM + 1], I32)
        cnt_i = sb("cnt_i", [1, 1], I32)

        xt = sb("xt", [P, 2, 2, D])
        xT = sb("xT", [P, 2, 512])
        kvs = sb("kvs", [P, 2, 2, 2 * D])

        dst_l = sb("dst_l", [P, 2, G + 2], I32)
        src_l = sb("src_l", [P, 2, G], I32)
        rel = sb("rel", [P, 2, G + 2])
        nbc = sb("nbc", [P, 1])
        nwc = sb("nwc", [P, 2])
        off_w = sb("off_w", [P, G])
        gidx = sb("gidx", [P, 2, G], I32)
        kv = sb("kv", [P, 2, G, 2 * D])
        onehot = sb("onehot", [P, 2, G, P])
        onehotT = sb("onehotT", [P, 2, G, P])
        assert RC <= G * P
        cmp = onehotT[:, 0].rearrange("p g k -> p (g k)")
        drow = onehotT[:, 1].rearrange("p g k -> p (g k)").bitcast(I32)[:, 0:RC]
        same = sb("same", [P, G + 1])
        msk = sb("msk", [P, G + 1])
        runs = sb("runs", [P, 2, H * G + 1])
        headm = sb("headm", [P, 2, 2, G])
        lastedge = sb("lastedge", [P, 2, G])
        one_run = sb("one_run", [P, 1])
        link = sb("link", [P, 2])
        mlc = sb("mlc", [P, 2, H])
        mlT = sb("mlT", [H, 2, 2 * P])
        xw = sb("xw", [P, 2, D])
        xwT = sb("xwT", [P, D])
        qf = sb("qf", [P, 2, D])
        res = sb("res", [P, 2, D])
        prod = sb("prod", [P, 2, 4, D])
        score = sb("score", [P, H, G])
        fmax = sb("fmax", [P, H, G])
        xs = sb("xs", [P, P + 1])
        ys = sb("ys", [P, P + 1])
        bmax = sb("bmax", [P, H, G])
        tu = sb("tu", [P, 2, H, G])
        m2 = sb("m2", [P, 2, H])
        mrun = sb("mrun", [P, H])
        pres = sb("pres", [P, 1])
        dab = sb("dab", [P, 2, H])
        ab = sb("ab", [P, 2, H])
        dexp = sb("dexp", [P, G, H])
        state = sb("state", [P, H, DK + 1])
        part = sb("part", [P, H, DK + 1])
        cell = sb("cell", [P, 16])
        zz = sb("zz", [P, 2, H])
        tn = sb("tn", [P, D])
        tT = sb("tT", [P, D])
        yy = sb("yy", [P, D])
        scratch = sb("scratch", [P, D])
        eps_c = sb("eps_c", [P, 1])
        ln = sb("ln", [P, 10])
        outb = sb("outb", [P, 2, D])

        wts_in = sem("wts_in")
        row_in = sem("row_in")
        drow_in = sem("drow_in")
        pads_in = sem("pads_in")
        consts = sem("consts")
        rz = sem("rz")
        pool_step = sem("pool_step")
        pad_tile = sem("pad_tile")
        dve_setup = sem("dve_setup")
        fold_in = sem("fold_in")
        fold_mm = sem("fold_mm")
        fold_cp = sem("fold_cp")
        skip_exp = sem("skip_exp")
        tab_mm = sem("tab_mm")
        tab_in = sem("tab_in")
        rows_idx = sem("rows_idx")
        tables = sem("tables")
        kv_clear = sem("kv_clear")
        x_in = [sem("x_in0"), sem("x_in1")]
        x_T = sem("x_T")
        x_Tc = sem("x_Tc")
        kv_mm = sem("kv_mm")
        kv_add = sem("kv_add")
        kv_out = [sem("kv_out0"), sem("kv_out1")]
        idx_in = sem("idx_in")
        xw_in = [sem("xw_in0"), sem("xw_in1")]
        e1_done = sem("e1_done")
        gat = [[sem(f"gat{b}_{q}") for q in range(NQ)] for b in range(2)]
        q_edge = sem("q_edge")
        q_used = sem("q_used")
        oh_dist = sem("oh_dist")
        oh_ready = sem("oh_ready")
        oh_T = sem("oh_T")
        oh_Tc = sem("oh_Tc")
        mask_T = sem("mask_T")
        win_T = sem("win_T")
        win_Tc = sem("win_Tc")
        win_q = sem("win_q")
        q_done = sem("q_done")
        x_scaled = sem("x_scaled")
        res_done = sem("res_done")
        masks_ready = sem("masks_ready")
        tail_ready = sem("tail_ready")
        tail_T = sem("tail_T")
        across_ready = sem("across_ready")
        carry_T = sem("carry_T")
        d_ready = sem("d_ready")
        ex_ready = sem("ex_ready")
        dab_ready = sem("dab_ready")
        ab_ready = sem("ab_ready")
        w_ready = sem("w_ready")
        agg_done = sem("agg_done")
        agg_read = sem("agg_read")
        tn_ready = sem("tn_ready")
        tn_T = sem("tn_T")
        tn_Tc = sem("tn_Tc")
        y_mm = sem("y_mm")
        yy_ready = sem("yy_ready")
        ln_step = sem("ln_step")
        rs_ready = sem("rs_ready")
        norm_ready = sem("norm_ready")
        fin_done = sem("fin_done")
        out_done = sem("out_done")
        dstep = sem("dstep")

        def bc(ap, axis, n):
            shape = list(ap.shape)
            return ap.unsqueeze(axis).to_broadcast(shape[:axis] + [n] + shape[axis:])

        def heads(ap):
            dims = " ".join("abc"[:len(ap.shape) - 1])
            return ap.rearrange(f"{dims} (h d) -> {dims} h d", h=H)

        def turns(eng):
            eng.wait_ge(tables, 1)
            return eng.value_load(cnt_i[0:1, 0:1], min_val=1, max_val=SM // 2 - 1)

        N_WTS = 16 * (4 + 4 + HPB + 1 + 2 * HPB)
        N_CONST = 12

        def rows2(t, base):
            d = t.shape[1]
            return bass.AP(t.tensor, base, [[2 * d, P], [d, 2], [1, d]])

        def rows1(t, base):
            return bass.AP(t.tensor, base, [[t.shape[1], P], [1, t.shape[1]]])

        STEP = 2 * P * D

        block = ctx.enter_context(nc.Block())

        @block.sync
        def _(sp):
            sp.dma_start(row1[0:1, 0:ROWS], bass.AP(dst.tensor, 0, [[RC, 1], [RC, ROWS]]),
                         allow_slow_non_contiguous=True).then_inc(row_in, 16)
            for k, wm in enumerate((Wk, Wv, Wq, Wa)):
                sp.dma_start(wl[:, k], wm.rearrange("(a p) i -> p a i", p=P)).then_inc(wts_in, 16)
            for k, bm in enumerate((bk, bv, bq, ba)):
                sp.dma_start(bcol[:, k], bm.rearrange("(a p) -> p a", p=P),
                             allow_slow_non_contiguous=True).then_inc(wts_in, 16)
            for q in range(HPB):
                sp.dma_start(pcol[DK * q:DK * q + DK, :],
                             bass.AP(rel_pri.tensor, q, [[0, DK], [HPB, 2]]),
                             allow_slow_non_contiguous=True).then_inc(wts_in, 16)
            sp.dma_start(skc[:, 0:1], bass.AP(skip.tensor, 0, [[0, P], [1, 1]])).then_inc(wts_in, 16)
            sp.wait_ge(rz, 1)
            for k, rm in enumerate((rel_att, rel_msg)):
                for q in range(HPB):
                    sp.dma_start(rfold[DK * q:DK * q + DK, k, :, DK * q:DK * q + DK],
                                 rm.rearrange("(a q) d e -> q d a e", q=HPB)[q]).then_inc(wts_in, 16)
            for k, (pad, arr) in enumerate(((dst_pad, dst), (src_pad, src))):
                sp.dma_start(pad[1:1 + E].rearrange("(a b) -> a b", a=16),
                             arr.rearrange("(a b) -> a b", a=16)).then_inc(pads_in, 16)
            sp.wait_ge(pad_tile, 2)
            for k, pad in enumerate((dst_pad, src_pad)):
                sp.dma_start(pad[0:1].rearrange("(a b) -> a b", a=1), padi[0:1, 0:1]).then_inc(pads_in, 16)
                sp.dma_start(pad[1 + E:EP].rearrange("(a b) -> a b", a=16),
                             padi[:, k * (TAIL // 16):(k + 1) * (TAIL // 16)]).then_inc(pads_in, 16)

            def load_tile(t, base):
                sp.wait_ge(x_T, t.done())
                sp.dma_start(xt[:, t.par], rows2(x, base)).then_inc(x_in[t.par], 16)

            load_tile(Chunk(0, 0), 0)
            load_tile(Chunk(0, 1), STEP)
            with sp.Fori(0, PL - 1) as i:
                for b in range(2):
                    x_next = sp.snap(i * (2 * STEP) + (b + 2) * STEP)
                    load_tile(Chunk(i, b + 2), x_next)
            load_tile(Chunk(PL, 0), (N - 2 * P) * D)

            n = turns(sp)
            sp.wait_ge(pads_in, 96)

            def load_chunk(c, s):
                first = sp.value_load(base_i[0:1, bass.ds(s, 1)], min_val=0, max_val=EP - C - 2)
                second = sp.snap(first + 1)
                node = sp.value_load(nb_i[0:1, bass.ds(s + 1, 1)], min_val=0, max_val=(N - P) * D)
                sp.wait_ge(e1_done, c.done())
                sp.nop(nofuse=True)
                sp.dma_start(dst_l[:, c.par], bass.AP(dst_pad.tensor, first, [[G, P], [1, G + 2]]))\
                    .then_inc(idx_in, 16)
                sp.dma_start(src_l[:, c.par], bass.AP(src_pad.tensor, second, [[G, P], [1, G]]))\
                    .then_inc(idx_in, 16)
                sp.wait_ge(res_done, c.done())
                sp.nop(nofuse=True)
                sp.dma_start(xw[:, c.par], rows1(x, node)).then_inc(xw_in[c.par], 16)

            def store_window(c, s):
                node = sp.value_load(nb_i[0:1, bass.ds(s, 1)], min_val=0, max_val=(N - P) * D)
                sp.wait_ge(fin_done, c.done(credit=2))
                sp.nop(nofuse=True)
                sp.wait_ge(out_done, c.done(per=16, credit=32))
                sp.nop(nofuse=True)
                sp.dma_start(rows1(out, node), outb[:, c.par]).then_inc(out_done, 16)

            load_chunk(Chunk(0, 0), 0)
            load_chunk(Chunk(0, 1), 1)
            with sp.Fori(0, n) as i:
                for b in range(2):
                    c = Chunk(i, b)
                    load_chunk(c.next().next(), 2 * i + b + 2)
                    store_window(c.prev(), 2 * i + b)
            store_window(Chunk(n, -1), 2 * n)
            sp.wait_ge(out_done, n * 32 + 48)
            sp.nop(nofuse=True)

        @block.gpsimd
        def _(pool):
            step = [0]

            def after(ins):
                step[0] += 1
                ins.then_inc(pool_step, 1)
                pool.wait_ge(pool_step, step[0])

            pool.memset(padi[:, 0:TAIL // 16], 1 << 20).then_inc(pad_tile, 1)
            pool.memset(padi[:, TAIL // 16:], 0).then_inc(pad_tile, 1)
            pool.memset(rfold[:, :, :, :], 0.0).then_inc(rz, 1)
            pool.memset(ones[:, :], 1.0).then_inc(consts, 1)
            after(pool.memset(ident[:, :], 0.0))
            pool.affine_select(out=ident[:, :], in_=ident[:, :], compare_op=ALU.not_equal, fill=1.0,
                               base=0, pattern=[[-1, P]], channel_multiplier=1).then_inc(consts, 1)
            pool.iota(thr[:, 0:1], pattern=[[0, 1]], base=0, channel_multiplier=P,
                      allow_small_or_imprecise_dtypes=True).then_inc(consts, 1)
            pool.iota(thr[:, 1:2], pattern=[[0, 1]], base=0, channel_multiplier=1,
                      allow_small_or_imprecise_dtypes=True).then_inc(consts, 1)
            pool.iota(iota_s[:, :], pattern=[[1, SM]], base=0, channel_multiplier=0,
                      allow_small_or_imprecise_dtypes=True).then_inc(consts, 1)
            pool.iota(iota_c[:, :], pattern=[[C, J]], base=C, channel_multiplier=0,
                      allow_small_or_imprecise_dtypes=True).then_inc(consts, 1)
            pool.iota(iota_n[:, :], pattern=[[1, P]], base=0, channel_multiplier=0,
                      allow_small_or_imprecise_dtypes=True).then_inc(consts, 1)
            after(pool.memset(lower[:, :], 1.0))
            pool.affine_select(out=lower[:, :], in_=lower[:, :], compare_op=ALU.is_gt, fill=0.0,
                               base=0, pattern=[[1, P]], channel_multiplier=-1).then_inc(consts, 1)
            after(pool.memset(diff[:, :], 0.0))
            after(pool.affine_select(out=diff[:, :], in_=diff[:, :], compare_op=ALU.not_equal, fill=1.0,
                                    base=-1, pattern=[[-1, P]], channel_multiplier=1))
            pool.affine_select(out=diff[:, :], in_=diff[:, :], compare_op=ALU.not_equal, fill=-1.0,
                               base=0, pattern=[[-1, P]], channel_multiplier=1).then_inc(consts, 1)
            after(pool.memset(lastw[:, :], 0.0))
            pool.affine_select(out=lastw[:, :], in_=lastw[:, :], compare_op=ALU.not_equal, fill=1e6,
                               base=1 - W, pattern=[[0, 1]], channel_multiplier=1).then_inc(consts, 1)
            after(pool.memset(ends[:, :], 1.0))
            pool.affine_select(out=ends[:, 0:1], in_=ends[:, 0:1], compare_op=ALU.not_equal, fill=0.0,
                               base=0, pattern=[[0, 1]], channel_multiplier=1).then_inc(consts, 1)
            pool.affine_select(out=ends[:, 1:2], in_=ends[:, 1:2], compare_op=ALU.not_equal, fill=0.0,
                               base=1 - P, pattern=[[0, 1]], channel_multiplier=1).then_inc(consts, 1)
            pool.wait_ge(rows_idx, 1)
            pool.indirect_dma_start(out=drow[:, :], out_offset=None,
                                    in_=dst.rearrange("(a b) -> a b", b=RC),
                                    in_offset=bass.IndirectOffsetOnAxis(ap=rowi[:, 0:1], axis=0),
                                    bounds_check=ROWS - 1, oob_is_err=False).then_inc(drow_in, 16)
            for b in range(2):
                pool.memset(kv[:, b], 0.0).then_inc(kv_clear, 1)
            pool.wait_ge(kv_out[0], 16 * (PL + 2))
            pool.wait_ge(kv_out[1], 16 * (PL + 1))
            pool.wait_ge(kv_clear, 2)
            n = turns(pool)
            last_row = pool.to_reg(N - 1)

            def gather(c):
                pool.wait_ge(e1_done, c.done(credit=1))
                pool.nop(nofuse=True)
                for q, (g0, gn) in enumerate(PAIRS):
                    if q % 2 == 0:
                        pool.wait_ge(w_ready, c.done(per=NT, credit=q // 2 + 1, back=NT))
                        pool.nop(nofuse=True)
                    for g in range(g0, g0 + gn):
                        pool.indirect_dma_start(
                            out=kv[:, c.par, g, :], out_offset=None, in_=kv_dram,
                            in_offset=bass.IndirectOffsetOnAxis(ap=gidx[:, c.par, g:g + 1], axis=0),
                            bounds_check=last_row, oob_is_err=False).then_inc(gat[c.par][q], 16)

            def residual(c):
                pool.wait_ge(xw_in[c.par], c.landed())
                pool.wait_ge(win_T, c.done())
                pool.wait_ge(fin_done, c.done())
                pool.nop(nofuse=True)
                pool.tensor_scalar(res[:, c.par], xw[:, c.par], skc[:, 4:5], None, ALU.mult).then_inc(x_scaled, 1)
                pool.wait_ge(x_scaled, c.done())
                pool.nop(nofuse=True)
                pool.tensor_tensor(res[:, c.par], res[:, c.par], bab[:, :], ALU.add).then_inc(res_done, 1)

            gather(Chunk(0, 0))
            with pool.Fori(0, n) as i:
                for b in range(2):
                    gather(Chunk(i, b).next())
                    residual(Chunk(i, b))

        @block.tensor
        def _(pe):
            pe.wait_ge(consts, N_CONST)
            pe.wait_ge(tab_in, 1)
            nc.tensor.matmul(bank[0][:, 0:ROWS], ones[0:1, :], rowf[0:1, 0:ROWS], start=True, stop=True)\
                .then_inc(tab_mm, 1)
            pe.wait_ge(tab_in, 2)
            nc.tensor.matmul(bank[1][:, 0:1], diff[:, :], tcol[:, 2:3], start=True, stop=True).then_inc(tab_mm, 1)
            pe.wait_ge(tab_in, 3)
            nc.tensor.matmul(bank[2][:, 0:1], lower[0:W, :], tcol[0:W, 4:5], start=True, stop=True)
            nc.tensor.matmul(bank[2][:, 1:2], ones[0:W, :], tcol[0:W, 4:5], start=True, stop=True)\
                .then_inc(tab_mm, 1)
            pe.wait_ge(tab_in, 4)
            nc.tensor.matmul(bank[3][:, 0:SM], cmp[0:W, 0:P], act_a[0:W, :], start=True, stop=True)
            nc.tensor.matmul(bank[4][:, 0:SM], cmp[0:W, P:2 * P], act_a[0:W, :], start=True, stop=True)\
                .then_inc(tab_mm, 1)

            pe.wait_ge(tables, 1)
            pe.wait_ge(wts_in, N_WTS)
            pe.wait_ge(fold_in, 1)
            for k in range(4):
                for a in range(2):
                    r = rfold[:, k, a] if k < 3 else ident[:, :]
                    for kh in range(2):
                        nc.tensor.matmul(bank[2 * k][:, kh * D + a * P:kh * D + (a + 1) * P],
                                         wl[:, k, a, kh * P:(kh + 1) * P], r, start=True, stop=True)
                    last = nc.tensor.matmul(bank[2 * k + 1][:, a * P:(a + 1) * P], bwide[:, k, a], r,
                                            start=True, stop=True)
                last.then_inc(fold_mm, 1)

            def transpose_x(t):
                pe.wait_ge(x_in[t.par], t.landed())
                pe.wait_ge(x_Tc, t.done())
                for j in range(2):
                    for kh in range(2):
                        last = nc.tensor.transpose(bank[t.par][:, (2 * j + kh) * P:(2 * j + kh + 1) * P],
                                                   xt[:, t.par, j, kh * P:(kh + 1) * P], ident[:, :])
                last.then_inc(x_T, 1)

            def project(t):
                pe.wait_ge(x_Tc, t.done(credit=2))
                pe.wait_ge(kv_add, t.done())
                for j in range(2):
                    for kh in range(2):
                        last = nc.tensor.matmul(bank[2 + 2 * t.par + j][:, :],
                                                xT[:, t.par, (2 * j + kh) * P:(2 * j + kh + 1) * P],
                                                wkv[:, kh], start=(kh == 0), stop=(kh == 1))
                last.then_inc(kv_mm, 1)

            pe.wait_ge(fold_cp, 4)
            transpose_x(Chunk(0, 0))
            with pe.Fori(0, PL) as i:
                for b in range(2):
                    transpose_x(Chunk(i, b).next())
                    project(Chunk(i, b))
            project(Chunk(PL, 0))
            pe.wait_ge(kv_add, 2 * PL + 3)

            def window_q_T(c):
                pe.wait_ge(xw_in[c.par], c.landed())
                pe.wait_ge(q_done, c.done(credit=1))
                for kh in range(2):
                    last = nc.tensor.transpose(ps_win[:, kh * P:(kh + 1) * P], xw[:, c.par, kh * P:(kh + 1) * P],
                                               ident[:, :])
                last.then_inc(win_T, 1)

            def window_q_mm(c):
                pe.wait_ge(win_Tc, c.done())
                for kh in range(2):
                    last = nc.tensor.matmul(ps_win[:, D:2 * D], xwT[:, kh * P:(kh + 1) * P], wq[:, kh],
                                            start=(kh == 0), stop=(kh == 1))
                last.then_inc(win_q, 1)

            def spread_q(c, q):
                if q == 0:
                    pe.wait_ge(q_done, c.done(credit=2))
                pe.wait_ge(q_used, c.done(per=NQ, credit=q + 1, back=NQ))
                g0, gn = PAIRS[q]
                if g0 % 4 == 0:
                    pe.wait_ge(oh_Tc, c.done(per=NT, credit=2 + g0 // 4 + 1, back=NT))
                for g in range(g0, g0 + gn):
                    last = nc.tensor.matmul(ps_q[(c.par + q) % 2][:, (g - g0) * D:(g - g0 + 1) * D],
                                            onehotT[:, c.par, g], qf[:, c.par], start=True, stop=True)
                last.then_inc(q_edge, 1)

            def transpose_onehots(c, t):
                g0, gn = FOURS[t]
                pe.wait_ge(oh_ready, c.done(per=NT, credit=t + 1, back=NT))
                if t == NT - 1:
                    pe.wait_ge(masks_ready, c.done())
                pe.wait_ge(oh_Tc, c.done(per=NT, credit=t + 1, back=NT))
                for g in range(g0, g0 + gn):
                    last = nc.tensor.transpose(ps_t[(c.par + t) % 2][:, (g - g0) * P:(g - g0 + 1) * P],
                                               onehot[:, c.par, g], ident[:, :])
                if t == NT - 1:
                    for m in range(2):
                        last = nc.tensor.transpose(ps_t[(c.par + t) % 2][0:H, (m + 2) * P:(m + 3) * P],
                                                   mlc[:, m], ident[:, :])
                last.then_inc(oh_T, 1)

            def finish_T(c):
                pe.wait_ge(tn_ready, c.done(credit=1))
                for kh in range(2):
                    last = nc.tensor.transpose(ps_fin[:, kh * P:(kh + 1) * P], tn[:, kh * P:(kh + 1) * P],
                                               ident[:, :])
                last.then_inc(tn_T, 1)

            def finish_mm(c):
                pe.wait_ge(tn_Tc, c.done(credit=1))
                for kh in range(2):
                    last = nc.tensor.matmul(ps_fin[:, D:2 * D], tT[:, kh * P:(kh + 1) * P], wa[:, kh],
                                            start=(kh == 0), stop=(kh == 1))
                last.then_inc(y_mm, 1)

            def aggregate(c, q):
                if q % 2 == 0:
                    pe.wait_ge(w_ready, c.done(per=NT, credit=NT + q // 2 + 1))
                g0, gn = PAIRS[q]
                for g in range(g0, g0 + gn):
                    last = nc.tensor.matmul(ps_agg[:, 0:WX], onehot[:, c.par, g], wv[:, g],
                                            start=(g == 0), stop=(g == G - 1))
                if q % 2 == 1 or q == NQ - 1:
                    last.then_inc(agg_done, 1)

            c0 = Chunk(0, 0)
            window_q_T(c0)
            window_q_mm(c0)
            transpose_onehots(c0, 0)
            transpose_onehots(c0, 1)
            window_q_T(c0.next())
            window_q_mm(c0.next())
            for t in range(2, NT):
                transpose_onehots(c0, t)
            for q in range(NQ):
                spread_q(c0, q)
            transpose_onehots(c0.next(), 0)
            transpose_onehots(c0.next(), 1)
            spread_q(c0.next(), 0)
            n = turns(pe)
            with pe.Fori(0, n) as i:
                for b in range(2):
                    c = Chunk(i, b)
                    prev, next1, next2 = c.prev(), c.next(), c.next().next()
                    pe.wait_ge(tail_ready, c.done())
                    nc.tensor.transpose(TAILT, bmax[:, :, G - 1], ident[:, :])
                    nc.tensor.transpose(HEADT, bmax[:, :, 0], ident[:, :]).then_inc(tail_T, 1)
                    transpose_onehots(next1, 2)
                    pe.wait_ge(across_ready, c.done())
                    nc.tensor.transpose(CARRYT[0], xs[:, 0:P], ident[:, :])
                    nc.tensor.transpose(CARRYT[1], ys[:, 1:P + 1], ident[:, :]).then_inc(carry_T, 1)
                    transpose_onehots(next1, 3)
                    transpose_onehots(next1, 4)
                    spread_q(next1, 1)
                    finish_T(prev)
                    finish_mm(prev)
                    pe.wait_ge(agg_read, c.done())
                    for q in range(NQ):
                        aggregate(c, q)
                        if q + 2 < NQ:
                            spread_q(next1, q + 2)
                        if q == 3:
                            window_q_T(next2)
                        if q == 4:
                            transpose_onehots(next2, 0)
                        if q == 6:
                            window_q_mm(next2)
                            transpose_onehots(next2, 1)
                    spread_q(next2, 0)
            finish_T(Chunk(n, -1))
            finish_mm(Chunk(n, -1))

        @block.scalar
        def _(act):
            act.wait_ge(wts_in, N_WTS)
            nc.scalar.activation(skc[:, 1:2], skc[:, 0:1], ACT.Exp, scale=-1.0).then_inc(skip_exp, 1)

            def copy_xT(t):
                act.wait_ge(x_T, t.done(credit=2))
                act.wait_ge(kv_mm, t.done())
                nc.scalar.activation(xT[:, t.par], bank[t.par][:, :], ACT.Copy).then_inc(x_Tc, 1)

            def store_tile(t, base):
                act.wait_ge(kv_add, t.done(credit=2))
                act.dma_start(rows2(kv_dram, base), kvs[:, t.par]).then_inc(kv_out[t.par], 16)

            copy_xT(Chunk(0, 0))
            with act.Fori(0, PL) as i:
                for b in range(2):
                    kv_here = act.snap(i * (4 * STEP) + b * 2 * STEP)
                    copy_xT(Chunk(i, b).next())
                    store_tile(Chunk(i, b), kv_here)
            act.wait_ge(kv_out[1], 16 * (PL + 1))
            store_tile(Chunk(PL, 0), (N - 2 * P) * 2 * D)

            def copy_xwT(c):
                act.wait_ge(win_T, c.done())
                nc.scalar.activation(xwT[:, :], ps_win[:, 0:D], ACT.Copy).then_inc(win_Tc, 1)

            def copy_onehotT(c, t):
                g0, gn = FOURS[t]
                act.wait_ge(oh_T, c.done(per=NT, credit=t + 1, back=NT))
                src_bank = ps_t[(c.par + t) % 2]
                if t == NT - 1:
                    nc.scalar.activation(mlT[:, c.par], src_bank[0:H, 2 * P:4 * P], ACT.Copy).then_inc(mask_T, 1)
                nc.scalar.activation(onehotT[:, c.par, g0:g0 + gn].rearrange("p g k -> p (g k)"),
                                     src_bank[:, 0:gn * P], ACT.Copy).then_inc(oh_Tc, 1)

            def one_hots(c, t):
                g0, gn = FOURS[t]
                for g in range(g0, g0 + gn):
                    last = nc.scalar.activation(onehot[:, c.par, g], iota_n[:, :], ACT.Abs,
                                                bias=rel[:, c.par, g + 1:g + 2])
                last.then_inc(oh_dist, 1)
                act.wait_ge(oh_dist, c.done(per=NT, credit=t + 1, back=NT))
                group = onehot[:, c.par, g0:g0 + gn].rearrange("p g k -> p (g k)")
                nc.scalar.activation(group, group, ACT.Relu, scale=-1.0, bias=ones[:, 0:1]).then_inc(oh_ready, 1)

            def copy_tT(c):
                act.wait_ge(tn_T, c.done(credit=1))
                nc.scalar.activation(tT[:, :], ps_fin[:, 0:D], ACT.Copy).then_inc(tn_Tc, 1)

            def statistics(c):
                act.wait_ge(yy_ready, c.done(credit=1))
                nc.scalar.activation(scratch[:, :], yy[:, :], ACT.Copy, accum_out=ln[:, 0:1]).then_inc(ln_step, 1)
                act.wait_ge(ln_step, c.done(per=4, credit=1))
                nc.scalar.activation(ln[:, 1:2], ln[:, 0:1], ACT.Copy, scale=-1.0 / D).then_inc(ln_step, 1)
                act.wait_ge(ln_step, c.done(per=4, credit=2))
                nc.scalar.activation(scratch[:, :], yy[:, :], ACT.Square, bias=ln[:, 1:2],
                                     accum_out=ln[:, 2:3]).then_inc(ln_step, 1)
                act.wait_ge(ln_step, c.done(per=4, credit=3))
                nc.scalar.activation(ln[:, 3:4], ln[:, 2:3], ACT.Ln, bias=eps_c[:, :], scale=1.0 / D)\
                    .then_inc(ln_step, 1)
                act.wait_ge(ln_step, c.done(per=4, credit=4))
                nc.scalar.activation(ln[:, 4:5], ln[:, 3:4], ACT.Exp, scale=-0.5).then_inc(rs_ready, 1)

            def merge_factors(c):
                act.wait_ge(dab_ready, c.done(credit=1))
                nc.scalar.activation(ab[:, :, :], dab[:, :, :], ACT.Exp).then_inc(ab_ready, 1)

            def weights(c):
                act.wait_ge(d_ready, c.done())
                nc.scalar.activation(heads(wv[:, :, 0:WC])[:, :, :, DK], dexp[:, :, :], ACT.Exp)\
                    .then_inc(ex_ready, 1)

            def layer_norm(c):
                act.wait_ge(norm_ready, c.done(credit=1))
                act.wait_ge(out_done, c.done(per=16, credit=16))
                nc.scalar.activation(outb[:, c.par], yy[:, :], ACT.Identity, scale=ln[:, 8:9], bias=ln[:, 9:10])\
                    .then_inc(fin_done, 1)

            c0 = Chunk(0, 0)
            copy_xwT(c0)
            act.wait_ge(e1_done, c0.done(credit=1))
            for t in range(NT):
                if t == 2:
                    copy_xwT(c0.next())
                one_hots(c0, t)
                copy_onehotT(c0, t)
            act.wait_ge(e1_done, c0.next().done(credit=1))
            for t in range(4):
                one_hots(c0.next(), t)
            copy_onehotT(c0.next(), 0)
            copy_onehotT(c0.next(), 1)
            n = turns(act)
            with act.Fori(0, n) as i:
                for b in range(2):
                    c = Chunk(i, b)
                    prev, next1, next2 = c.prev(), c.next(), c.next().next()

                    def next_one_hots(c, t):
                        act.wait_ge(agg_done, c.done(per=NT, credit=t + 1, back=NT))
                        one_hots(c, t)

                    merge_factors(prev)
                    next_one_hots(next1, 4)
                    copy_onehotT(next1, 2)
                    weights(c)
                    copy_onehotT(next1, 3)
                    copy_tT(prev)
                    copy_onehotT(next1, 4)
                    statistics(prev)
                    act.wait_ge(e1_done, next2.done(credit=1))
                    next_one_hots(next2, 0)
                    copy_xwT(next2)
                    next_one_hots(next2, 1)
                    copy_onehotT(next2, 0)
                    next_one_hots(next2, 2)
                    copy_onehotT(next2, 1)
                    layer_norm(prev)
                    next_one_hots(next2, 3)
            merge_factors(Chunk(n, -1))
            copy_tT(Chunk(n, -1))
            statistics(Chunk(n, -1))
            layer_norm(Chunk(n, -1))

        @block.vector
        def _(v):
            step = [0]

            def after(ins):
                step[0] += 1
                ins.then_inc(dve_setup, 1)
                v.wait_ge(dve_setup, step[0])

            v.wait_ge(consts, N_CONST)
            v.wait_ge(row_in, 16)
            after(v.memset(rowf[:, :], 0.0))
            after(v.tensor_copy(rowf[0:1, 0:ROWS], row1[0:1, 0:ROWS]))
            after(v.tensor_scalar(tcol[:, 0:1], thr[:, 1:2], float(W), 1e6, ALU.is_ge, ALU.mult))
            after(v.tensor_scalar(tcol[:, 1:2], thr[:, 0:1], float(N - P), None, ALU.min))
            after(v.tensor_tensor(tcol[:, 0:1], tcol[:, 0:1], tcol[:, 1:2], ALU.add))
            v.memset(outb[:, :, :], 0.0).then_inc(tab_in, 1)
            v.wait_ge(tab_mm, 1)
            after(v.tensor_scalar(cmp[:, 0:ROWS], bank[0][:, 0:ROWS], tcol[:, 0:1], None, ALU.is_lt))
            after(v.tensor_reduce(tcol[:, 8:9], cmp[:, 0:ROWS], AX.X, ALU.add))
            after(v.tensor_scalar(tcol[:, 9:10], tcol[:, 8:9], -1.0, 0.0, ALU.add, ALU.max))
            v.tensor_copy(rowi[:, :], tcol[:, 9:10]).then_inc(rows_idx, 1)
            v.wait_ge(drow_in, 16)
            after(v.tensor_scalar(cmp[:, 0:RC], drow[:, :], tcol[:, 0:1], None, ALU.is_lt))
            after(v.tensor_reduce(tcol[:, 10:11], cmp[:, 0:RC], AX.X, ALU.add))
            v.scalar_tensor_tensor(out=tcol[:, 2:3], in0=tcol[:, 9:10], scalar=float(RC), in1=tcol[:, 10:11],
                                   op0=ALU.mult, op1=ALU.add).then_inc(tab_in, 1)
            v.wait_ge(tab_mm, 2)
            v.wait_ge(tab_in, 2)
            after(v.tensor_copy(tcol[:, 3:4], bank[1][:, 0:1]))
            after(v.tensor_scalar(cmp[:, 0:J], iota_c[:, :], tcol[:, 3:4], None, ALU.is_lt))
            after(v.tensor_reduce(tcol[:, 11:12], cmp[:, 0:J], AX.X, ALU.add))
            v.tensor_scalar(tcol[:, 4:5], tcol[:, 11:12], 1.0, None, ALU.add).then_inc(tab_in, 1)
            v.wait_ge(tab_mm, 3)
            v.wait_ge(tab_in, 3)
            after(v.tensor_copy(tcol[:, 5:6], bank[2][:, 0:1]))
            after(v.tensor_tensor(tcol[:, 12:13], tcol[:, 5:6], tcol[:, 4:5], ALU.add))
            after(v.tensor_tensor(tcol[:, 6:7], tcol[:, 12:13], lastw[:, :], ALU.add))
            after(v.tensor_scalar(act_b[:, :], iota_s[:, :], tcol[:, 6:7], None, ALU.is_ge))
            after(v.scalar_tensor_tensor(out=act_a[:, :], in0=iota_s[:, :], scalar=tcol[:, 5:6], in1=act_b[:, :],
                                        op0=ALU.is_ge, op1=ALU.subtract))
            after(v.scalar_tensor_tensor(out=tcol[:, 7:8], in0=tcol[:, 5:6], scalar=-float(C), in1=tcol[:, 2:3],
                                        op0=ALU.mult, op1=ALU.add))
            after(v.tensor_scalar(cmp[:, 0:P], ones[:, :], tcol[:, 0:1], None, ALU.mult))
            after(v.tensor_scalar(cmp[:, P:2 * P], ones[:, :], tcol[:, 7:8], None, ALU.mult))
            after(v.tensor_copy(tcol[:, 13:14], bank[2][:, 1:2]))
            after(v.tensor_scalar(act_b[:, 0:SM // 2], iota_s[:, 0:SM // 2], 2.0, tcol[:, 13:14], ALU.mult,
                                 ALU.is_lt))
            after(v.tensor_reduce(tcol[:, 14:15], act_b[:, 0:SM // 2], AX.X, ALU.add))
            after(v.tensor_copy(cnt_i[0:1, 0:1], tcol[0:1, 14:15]))
            v.memset(yy[:, :], 0.0).then_inc(tab_in, 1)
            v.wait_ge(tab_mm, 4)
            after(v.tensor_copy(nb_t[:, :], bank[3][:, 0:SM]))
            after(v.scalar_tensor_tensor(out=base_t[:, :], in0=iota_s[:, :], scalar=float(C), in1=bank[4][:, 0:SM],
                                        op0=ALU.mult, op1=ALU.add))
            after(v.tensor_copy(base_i[0:1, :], base_t[0:1, :]))
            after(v.memset(nb_i[0:1, 0:1], 0))
            after(v.tensor_scalar(nb_i[0:1, 1:SM + 1], nb_t[0:1, :], float(D), None, ALU.mult))
            after(v.memset(nw_t[:, :], -3 * BIG))
            after(v.tensor_tensor(nw_t[:, 1:SM], nb_t[:, 1:SM], nb_t[:, 0:SM - 1], ALU.is_equal))
            after(v.tensor_scalar(nw_t[:, 1:SM], nw_t[:, 1:SM], 3 * BIG, -3 * BIG, ALU.mult, ALU.add))
            after(v.memset(runs[:, :, :], -BIG))
            after(v.memset(nwc[:, :], 0.0))
            after(v.memset(eps_c[:, :], EPS))
            after(v.memset(mrun[:, :], -BIG))
            after(v.memset(state[:, :, :], 0.0))
            after(v.memset(ab[:, :, :], 0.0))
            after(v.memset(res[:, :, :], 0.0))
            for k, (s, by) in enumerate(((x_T, 2), (x_Tc, 2), (kv_mm, 2), (kv_out[0], 16), (kv_out[1], 16),
                          (kv_add, 2), (e1_done, 1), (q_done, 2), (res_done, 2), (out_done, 32),
                          (w_ready, 2 * NT), (q_used, 2),
                          (oh_Tc, 2), (agg_done, 2 * NT), (fin_done, 1))):
                v.memset(cell[:, k:k + 1], 0.0).then_inc(s, by)
            v.memset(cell[:, 15:16], 0.0).then_inc(tables, 1)

            v.wait_ge(wts_in, N_WTS)
            v.wait_ge(rz, 1)
            for k in range(4):
                for a in range(2):
                    after(v.tensor_copy(bwide[:, k, a], bcol[:, k, a:a + 1].to_broadcast([P, P])))
            for a in range(2):
                after(v.tensor_scalar(rfold[:, 2, a], ident[:, :], pcol[:, a:a + 1], 1.0 / math.sqrt(DK),
                                     ALU.mult, ALU.mult))
            after(v.memset(xs[:, :], 0.0))
            after(v.memset(ys[:, :], 0.0))
            after(v.memset(xs[0:H, :], -BIG))
            v.memset(ys[0:H, :], -BIG).then_inc(fold_in, 1)
            v.wait_ge(skip_exp, 1)
            after(v.tensor_scalar(skc[:, 2:3], skc[:, 1:2], 1.0, None, ALU.add))
            after(v.reciprocal(skc[:, 3:4], skc[:, 2:3]))
            after(v.tensor_scalar(skc[:, 4:5], skc[:, 3:4], -1.0, 2.0, ALU.mult, ALU.add))
            for k, (wt, off, bt) in enumerate(((wkv, 0, bkv), (wkv, D, bkv), (wq, 0, bqb), (wa, 0, bab))):
                v.wait_ge(fold_mm, k + 1)
                folded = bank[2 * k][:, :].rearrange("p (a c) -> p a c", a=2)
                if k < 3:
                    after(v.tensor_copy(wt[:, :, off:off + D], folded))
                    last = v.tensor_copy(bt[:, off:off + D], bank[2 * k + 1][:, 0:D])
                else:
                    after(v.tensor_scalar(wt[:, :, :], folded, skc[:, 3:4], None, ALU.mult))
                    last = v.tensor_scalar(bt[:, :], bank[2 * k + 1][:, 0:D], skc[:, 3:4], None, ALU.mult)
                last.then_inc(fold_cp, 1)

            def add_bias(t):
                v.wait_ge(kv_mm, t.done(credit=2))
                v.wait_ge(kv_out[t.par], t.landed())
                for j in range(2):
                    last = v.tensor_tensor(kvs[:, t.par, j], bank[2 + 2 * t.par + j][:, :], bkv[:, :], ALU.add)
                last.then_inc(kv_add, 1)

            with v.Fori(0, PL) as i:
                for b in range(2):
                    add_bias(Chunk(i, b))
            add_bias(Chunk(PL, 0))

            def lapped(ins):
                count[0] += 1
                ins.then_inc(dstep, 1)
                return count[0]

            def settle(c, k):
                v.wait_ge(dstep, c.done(per=K_DVE, credit=STEPS0 + k, back=K_DVE))

            def dlink(c, ins):
                settle(c, lapped(ins))

            mark = {}

            def edges_a(c):
                mark["nbc"] = lapped(v.tensor_copy(nbc[:, :], nb_t[:, bass.ds(c.number(), 1)]))

            def edges_b(c, at):
                v.wait_ge(idx_in, c.done(per=32))
                settle(at, mark["nbc"])
                mark["rel"] = lapped(v.tensor_scalar(rel[:, c.par], dst_l[:, c.par], nbc[:, :], -1.0,
                                                     ALU.subtract, ALU.mult))

            def edges_c(c, at):
                settle(at, mark["rel"])
                mark["off_w"] = lapped(v.tensor_scalar(off_w[:, :], rel[:, c.par, 1:G + 1], -float(P), FAR,
                                                       ALU.is_le, ALU.mult))

            def edges_d(c, at):
                settle(at, mark["off_w"])
                v.tensor_tensor(gidx[:, c.par], off_w[:, :], src_l[:, c.par], ALU.add).then_inc(e1_done, 1)

            def edges_in(c, at):
                edges_a(c)
                edges_b(c, at)
                edges_c(c, at)
                edges_d(c, at)

            def window_start(c):
                lapped(v.tensor_copy(nwc[:, c.par:c.par + 1], nw_t[:, bass.ds(c.number(), 1)]))

            def masks_a(c):
                p = c.par
                lapped(v.tensor_tensor(headm[:, p], bc(rel[:, p, 1:G + 1], 1, 2), bc(rel[:, p, 1:G + 1:G - 1], 2, G),
                                       ALU.is_equal))
                mark["same"] = lapped(v.tensor_tensor(same[:, :], rel[:, p, 1:G + 2], rel[:, p, 0:G + 1],
                                                      ALU.is_equal))

            def masks_b(at):
                settle(at, mark["same"])
                mark["ends"] = lapped(v.tensor_tensor(same[:, 0:G + 1:G], same[:, 0:G + 1:G], ends[:, :], ALU.mult))

            def masks_c(c, at):
                settle(at, mark["ends"])
                lapped(v.tensor_scalar(lastedge[:, c.par], same[:, 1:G + 1], -1.0, 1.0, ALU.mult, ALU.add))
                mark["msk"] = lapped(v.tensor_scalar(msk[:, :], same[:, :], BIG, -BIG, ALU.mult, ALU.add))

            def masks_d(c, at):
                settle(at, mark["msk"])
                lapped(v.tensor_scalar(link[:, :], msk[:, 0:G + 1:G], -BIG, None, ALU.add))
                lapped(v.tensor_reduce(one_run[:, :], msk[:, 1:G], AX.X, ALU.min))
                inner = runs[:, c.par, 0:H * G].rearrange("p (h g) -> p h g", h=H)[:, :, 1:G]
                mark["runs"] = lapped(v.tensor_copy(inner, bc(msk[:, 1:G], 1, H)))

            def masks_e(c, at):
                settle(at, mark["runs"])
                lapped(v.scalar_tensor_tensor(out=headm[:, c.par], in0=headm[:, c.par], scalar=BIG,
                                              in1=bc(link[:, :], 2, G), op0=ALU.mult, op1=ALU.add))
                v.tensor_scalar(mlc[:, :, :], bc(msk[:, 0:G + 1:G], 2, H), one_run[:, :], None, ALU.add)\
                    .then_inc(masks_ready, 1)

            def window_q_in(c):
                v.wait_ge(win_q, c.done())
                v.tensor_tensor(qf[:, c.par], ps_win[:, D:2 * D], bqb[:, :], ALU.add).then_inc(q_done, 1)

            def multiply(c, q):
                g0, gn = PAIRS[q]
                v.wait_ge(gat[c.par][q], c.landed(per=16 * gn))
                v.wait_ge(q_edge, c.done(per=NQ, credit=q + 1, back=NQ))
                v.tensor_tensor(prod[:, q // 2 % 2, g0 % 4:g0 % 4 + gn], kv[:, c.par, g0:g0 + gn, 0:D],
                                ps_q[(c.par + q) % 2][:, 0:gn * D].rearrange("p (g d) -> p g d", d=D),
                                ALU.mult).then_inc(q_used, 1)

            def scores(c, t):
                g0, gn = FOURS[t]
                v.wait_ge(q_used, c.done(per=NQ, credit=2 + min(2 * t + 2, NQ), back=NQ))
                return lapped(v.tensor_reduce(score[:, :, g0:g0 + gn].rearrange("p h g -> p g h"),
                                              prod[:, t % 2, 0:gn].rearrange("p g (h d) -> p g h d", d=DK),
                                              AX.X, ALU.add))

            def merge_maxima_a(c):
                v.wait_ge(agg_done, c.done(per=NT, credit=2 * NT))
                lapped(v.tensor_scalar(m2[:, 0], mrun[:, :], nwc[:, c.par:c.par + 1], None, ALU.add))
                mark["pres"] = lapped(v.tensor_scalar(pres[:, :], NMAX[:, H:H + 1], BIG, -BIG, ALU.mult, ALU.add))

            def merge_maxima_b(at):
                settle(at, mark["pres"])
                mark["m2"] = lapped(v.tensor_scalar(m2[:, 1], NMAX[:, 0:H], pres[:, :], None, ALU.add))

            def merge_maxima_c(at):
                settle(at, mark["m2"])
                mark["mrun"] = lapped(v.tensor_tensor(mrun[:, :], m2[:, 0], m2[:, 1], ALU.max))

            def merge_maxima_d(at):
                settle(at, mark["mrun"])
                v.tensor_tensor(dab[:, :, :], m2[:, :, :], bc(mrun[:, :], 1, 2), ALU.subtract).then_inc(dab_ready, 1)

            def merge_a(c):
                v.wait_ge(ab_ready, c.done(credit=1))
                lapped(v.tensor_tensor(state[:, :, :], state[:, :, :], bc(ab[:, 0], 2, DK + 1), ALU.mult))
                v.tensor_tensor(part[:, :, :], heads(ps_agg[:, 0:WC]), bc(ab[:, 1], 2, DK + 1), ALU.mult)\
                    .then_inc(agg_read, 1)

            def merge_b(c, at):
                v.wait_ge(agg_read, c.done(credit=1))
                mark["state"] = lapped(v.tensor_tensor(state[:, :, :], state[:, :, :], part[:, :, :], ALU.add))

            def merge_c(at):
                settle(at, mark["state"])
                mark["zz"] = lapped(v.scalar_tensor_tensor(out=zz[:, 0], in0=state[:, :, DK], scalar=0.0,
                                                           in1=state[:, :, DK], op0=ALU.is_equal, op1=ALU.add))

            def merge_d(at):
                settle(at, mark["zz"])
                mark["1/zz"] = lapped(v.reciprocal(zz[:, 1], zz[:, 0]))

            def merge_e(at):
                settle(at, mark["1/zz"])
                v.tensor_tensor(tn[:, :].rearrange("p (h d) -> p h d", h=H), state[:, :, 0:DK],
                                bc(zz[:, 1], 2, DK), ALU.mult).then_inc(tn_ready, 1)

            def weigh(c, t):
                g0, gn = FOURS[t]
                if t == 0:
                    v.wait_ge(ex_ready, c.done())
                w4 = heads(wv[:, g0:g0 + gn, 0:WC])
                v.tensor_tensor(w4[:, :, :, 0:DK],
                                kv[:, c.par, g0:g0 + gn, D:2 * D].rearrange("p g (h d) -> p g h d", d=DK),
                                bc(w4[:, :, :, DK], 3, DK), ALU.mult).then_inc(w_ready, 1)

            def finish(c):
                v.wait_ge(y_mm, c.done(credit=1))
                v.wait_ge(res_done, c.done(credit=2))
                v.wait_ge(fin_done, c.done(credit=1))
                v.tensor_tensor(yy[:, :], ps_fin[:, D:2 * D], res[:, c.par], ALU.add).then_inc(yy_ready, 1)

            def normalise_a(c):
                v.wait_ge(rs_ready, c.done(credit=1))
                lapped(v.tensor_scalar(ln[:, 5:6], ln[:, 2:3], 1.0 / D, EPS, ALU.mult, ALU.add))
                mark["r2"] = lapped(v.tensor_tensor(ln[:, 6:7], ln[:, 4:5], ln[:, 4:5], ALU.mult))

            def normalise_b(at):
                settle(at, mark["r2"])
                mark["vr2"] = lapped(v.scalar_tensor_tensor(out=ln[:, 7:8], in0=ln[:, 6:7], scalar=-0.5,
                                                            in1=ln[:, 5:6], op0=ALU.mult, op1=ALU.mult))

            def normalise_c(at):
                settle(at, mark["vr2"])
                mark["rstd"] = lapped(v.scalar_tensor_tensor(out=ln[:, 8:9], in0=ln[:, 7:8], scalar=1.5,
                                                             in1=ln[:, 4:5], op0=ALU.add, op1=ALU.mult))

            def normalise_d(at):
                settle(at, mark["rstd"])
                v.tensor_tensor(ln[:, 9:10], ln[:, 1:2], ln[:, 8:9], ALU.mult).then_inc(norm_ready, 1)

            def flat(t):
                return t.rearrange("p h g -> p (h g)")

            def back(t, width, first, n, rows=None):
                return bass.AP(t, first, [[width, rows or t.shape[0]], [-1, n]])

            def maxima(c, at):
                b, prev = c.par, c.prev()
                forward = lapped(v.tensor_tensor_scan(flat(fmax[:, :, :]), runs[:, b, 0:H * G],
                                                      flat(score[:, :, :]), -BIG, ALU.add, ALU.max))
                merge_maxima_a(prev)
                settle(at, forward)
                v.tensor_tensor_scan(back(bmax, H * G, H * G - 1, H * G),
                                     back(runs, 2 * (H * G + 1), b * (H * G + 1) + H * G, H * G),
                                     back(fmax, H * G, H * G - 1, H * G), -BIG, ALU.add, ALU.max)\
                    .then_inc(tail_ready, 1)
                merge_maxima_b(at)
                edges_a(c.next().next())
                merge_maxima_c(at)
                window_start(c.next())
                merge_maxima_d(at)
                v.wait_ge(mask_T, c.done())
                v.wait_ge(tail_T, c.done())
                v.tensor_tensor_scan(xs[0:H, 1:P + 1], mlT[:, b, 0:P], TAILT, -BIG, ALU.add, ALU.max)
                v.tensor_tensor_scan(back(ys, P + 1, P - 1, P, H), back(mlT, 4 * P, (2 * b + 2) * P - 1, P),
                                     back(ps_small, 512, 2 * P - 1, P, H), -BIG, ALU.add, ALU.max)\
                    .then_inc(across_ready, 1)
                merge_a(prev)
                v.wait_ge(carry_T, c.done())
                carry = ps_small[:, 2 * P:4 * P].rearrange("p (k n) -> p k n", k=2)[:, :, 0:H]
                carried = lapped(v.tensor_tensor(tu[:, :, :, :], bc(carry, 3, G), bc(headm[:, b], 2, H), ALU.add))
                merge_b(prev, at)
                settle(at, carried)
                either = lapped(v.tensor_tensor(tu[:, 0], tu[:, 0], tu[:, 1], ALU.max))
                merge_c(at)
                settle(at, either)
                v.wait_ge(tail_ready, c.done())
                top = lapped(v.tensor_tensor(tu[:, 0], tu[:, 0], bmax[:, :, :], ALU.max))
                merge_d(at)
                settle(at, top)
                v.tensor_tensor(dexp[:, :, :], score[:, :, :].rearrange("p h g -> p g h"),
                                tu[:, 0].rearrange("p h g -> p g h"), ALU.subtract).then_inc(d_ready, 1)
                v.tensor_tensor(wv[:, :, WC:WC + H], tu[:, 0].rearrange("p h g -> p g h"), bc(lastedge[:, b], 2, H),
                                ALU.mult)
                merge_e(at)
                v.tensor_copy(wv[:, :, WX - 1], lastedge[:, b])

            count = [0]
            K_DVE, STEPS0 = 0, 0
            c0 = Chunk(0, 0)
            v.wait_ge(kv_add, 2 * PL + 3)
            dlink(c0, v.memset(ps_agg[:, :], 0.0))
            edges_in(c0, c0)
            edges_in(c0.next(), c0)
            window_start(c0)
            for c in (c0, c0.next()):
                masks_a(c)
                masks_b(c0)
                masks_c(c, c0)
                masks_d(c, c0)
                if c.off == 1:
                    v.wait_ge(mask_T, c0.done())
                masks_e(c, c0)
                window_q_in(c)

            def score_groups(c, at, before, between):
                reduced = []
                for q in range(NQ):
                    before(q)
                    if q >= 4:
                        settle(at, reduced[q // 2 - 2])
                    multiply(c, q)
                    between(q)
                    if q % 2 == 0 and q >= 2:
                        reduced.append(scores(c, q // 2 - 1))
                between(NQ)
                settle(at, scores(c, NT - 1))

            score_groups(c0, c0, lambda q: None, lambda q: None)
            K_DVE, STEPS0 = 34, count[0]
            n = turns(v)
            with v.Fori(0, n) as i:
                for b in range(2):
                    c = Chunk(i, b)
                    prev, next1, next2 = c.prev(), c.next(), c.next().next()
                    count[0] = 0
                    maxima(c, c)

                    def before(q):
                        if q % 2 == 0:
                            weigh(c, q // 2)
                        if q == 2:
                            edges_d(next2, c)
                            masks_b(c)
                        if q == 4:
                            masks_e(next2, c)
                        if q == 6:
                            normalise_c(c)

                    def between(q):
                        if q == 0:
                            edges_b(next2, c)
                        if q == 1:
                            edges_c(next2, c)
                            masks_a(next2)
                            finish(prev)
                        if q == 2:
                            masks_c(next2, c)
                        if q == 3:
                            masks_d(next2, c)
                        if q == 4:
                            normalise_a(prev)
                        if q == 5:
                            normalise_b(c)
                        if q == 6:
                            normalise_d(c)
                        if q == NQ:
                            window_q_in(next2)

                    score_groups(next1, c, before, between)
                    assert count[0] == K_DVE, count
            end = Chunk(n, -1)
            at = Chunk(n, 0)
            count[0] = 0
            merge_maxima_a(end)
            merge_maxima_b(at)
            merge_maxima_c(at)
            merge_maxima_d(at)
            merge_a(end)
            merge_b(end, at)
            merge_c(at)
            merge_d(at)
            merge_e(at)
            finish(end)
            normalise_a(end)
            normalise_b(at)
            normalise_c(at)
            normalise_d(at)


NAMES = ["x", "src", "dst", "L0_gnn_Wk", "L0_gnn_bk", "L0_gnn_Wq", "L0_gnn_bq", "L0_gnn_Wv", "L0_gnn_bv",
         "L0_gnn_Wa", "L0_gnn_ba", "L0_gnn_rel_att", "L0_gnn_rel_msg", "L0_gnn_rel_pri", "L0_gnn_skip"]


def kernel(**inputs):
    import numpy as np
    import concourse.bacc as bacc
    from concourse.bass_utils import run_bass_kernel_spmd

    nc = bacc.Bacc("TRN2", target_bir_lowering=False, num_devices=1)
    arrays, args = {}, []
    for name in NAMES:
        a = np.ascontiguousarray(inputs[name])
        a = a.reshape(1) if a.ndim == 0 else a
        arrays[name] = a
        args.append(nc.dram_tensor(name, a.shape, mybir.dt.from_np(a.dtype), kind="ExternalInput").ap())
    out = nc.dram_tensor("result", arrays["x"].shape, F32, kind="ExternalOutput").ap()
    gnn_program(nc, *args, out)
    return run_bass_kernel_spmd(nc, [arrays], core_ids=[0]).results[0]["result"]
```
